# Optimizing a Trainium2 kernel written in Bass

```python
import numpy as np
import jax
import jax.numpy as jnp

def _softmax(x, axis=-1):
    return jax.nn.softmax(x, axis=axis)

def _gelu(x):
    return jax.nn.gelu(x, approximate=True)

def _silu(x):
    return jax.nn.silu(x)

def _sigmoid(x):
    return jax.nn.sigmoid(x)

def _layernorm(x, axis=-1, eps=1e-05):
    m = jnp.mean(x, axis=axis, keepdims=True)
    v = jnp.var(x, axis=axis, keepdims=True)
    return (x - m) / jnp.sqrt(v + eps)

def _scatter_add(tgt, idx, src, axis=0):
    return tgt.at[idx].add(src)

def _segment_sum(src, seg, n):
    return jax.ops.segment_sum(src, seg, n)
kernel_name = 'mk_cond_resid_d1_seqx_r2_3a38c0'

def setup_inputs(seed: int=0):
    np.random.seed(seed)
    _w = jnp.asarray

    def _rec_inputs():
        import jax
        import jax.numpy as jnp
        _rk = jax.random.key(seed)
        x = -0.0003929 + 0.9999 * jax.random.normal(jax.random.fold_in(_rk, 1), (8, 1024, 512), jnp.float32)
        _lenS = 1024 - jax.random.randint(jax.random.fold_in(_rk, 7), (8,), 0, max(1, 1024 // 4) + 1, jnp.int32)
        _lenS2 = 1024 - jax.random.randint(jax.random.fold_in(_rk, 8), (8,), 0, max(1, 1024 // 4) + 1, jnp.int32)
        itok_BxS_2_50255 = jax.random.randint(jax.random.fold_in(_rk, 11), (8, 1024), 2, 25128, jnp.int32)
        cond_1024 = -0.00920427 + 1.00102 * jax.random.normal(jax.random.fold_in(_rk, 12), (8, 512), jnp.float32)
        return (x, itok_BxS_2_50255, cond_1024)
    x, itok_BxS_2_50255, cond_1024 = _rec_inputs()

    def _L0_cond_setup():
        import jax, jax.numpy as jnp
        import numpy as np
        HASH_PRIME = 5099
        MIN_CAPACITY = 4
        key = jax.random.key(seed)
        ks = jax.random.split(key, 8)
        B, T, D, F, E = (8, 1024, 512, 1024, 16)
        return {'x': jax.random.normal(ks[0], (B, T, D), dtype=jnp.float32), 'token_ids': jax.random.randint(ks[1], (B, T), 0, 50257, dtype=jnp.int32), 'shift_state': jax.random.normal(ks[2], (B, D), dtype=jnp.float32), 'time_maa_k': jax.random.uniform(ks[3], (D,), dtype=jnp.float32), 'time_maa_r': jax.random.uniform(ks[4], (D,), dtype=jnp.float32), 'w_recept': jax.random.normal(ks[5], (D, D), dtype=jnp.float32) * 0.02, 'w_key': jax.random.normal(ks[6], (E, D, F), dtype=jnp.float32) * 0.02, 'w_value': jax.random.normal(ks[7], (E, F, D), dtype=jnp.float32) * 0.02}
    _L0_cond_all = _L0_cond_setup()
    _L0_cond_in = {k: v for k, v in _L0_cond_all.items() if k in ('time_maa_k', 'time_maa_r', 'w_recept', 'w_key', 'w_value')}
    del _L0_cond_all
    return {'x': x, 'itok_BxS_2_50255': itok_BxS_2_50255, 'cond_1024': cond_1024, 'L0_cond_time_maa_k': _L0_cond_in['time_maa_k'], 'L0_cond_time_maa_r': _L0_cond_in['time_maa_r'], 'L0_cond_w_recept': _L0_cond_in['w_recept'], 'L0_cond_w_key': _L0_cond_in['w_key'], 'L0_cond_w_value': _L0_cond_in['w_value']}

def reference(x, itok_BxS_2_50255, cond_1024, L0_cond_time_maa_k, L0_cond_time_maa_r, L0_cond_w_recept, L0_cond_w_key, L0_cond_w_value):
    import jax
    import jax.numpy as jnp

    def _L0_cond_ref(x, token_ids, shift_state, time_maa_k, time_maa_r, w_recept, w_key, w_value):
        import jax, jax.numpy as jnp
        import numpy as np
        HASH_PRIME = 5099
        MIN_CAPACITY = 4
        B, T, D = x.shape
        E = w_key.shape[0]
        N = B * T
        C = max(MIN_CAPACITY, N // E)
        xprev = jnp.concatenate([shift_state[:, None, :], x[:, :-1]], axis=1)
        dxprev = xprev - x
        xk = x + dxprev * time_maa_k
        xr = x + dxprev * time_maa_r
        e_idx = token_ids.reshape(N).astype(jnp.int32) * HASH_PRIME % E
        onehot = (e_idx[:, None] == jnp.arange(E, dtype=jnp.int32)[None, :]).astype(jnp.int32)
        pos = jnp.take_along_axis(jnp.cumsum(onehot, axis=0), e_idx[:, None], axis=1)[:, 0] - 1
        keep = pos < C
        slot = jnp.where(keep, e_idx * C + pos, E * C)
        xk_flat = xk.reshape(N, D)
        buf = jnp.zeros((E * C + 1, D), dtype=x.dtype).at[slot].set(xk_flat)
        expert_in = buf[:E * C].reshape(E, C, D)
        h = jnp.square(jax.nn.relu(jnp.einsum('ecd,edf->ecf', expert_in, w_key)))
        expert_out = jnp.einsum('ecf,efd->ecd', h, w_value)
        out_pad = jnp.concatenate([expert_out.reshape(E * C, D), jnp.zeros((1, D), dtype=x.dtype)], axis=0)
        y = out_pad[slot].reshape(B, T, D)
        r = jax.nn.sigmoid(jnp.einsum('btd,ed->bte', xr, w_recept))
        return r * y
    x = x + _L0_cond_ref(x, itok_BxS_2_50255, cond_1024, L0_cond_time_maa_k, L0_cond_time_maa_r, L0_cond_w_recept, L0_cond_w_key, L0_cond_w_value)
    return x

_drawn_inputs = setup_inputs


def setup_inputs(seed=0):
    import zlib

    import numpy as np

    out = dict(_drawn_inputs(seed))
    spreads = {}
    factors = {'cond_1024': 8.0, 'L0_cond_time_maa_r': 8.0, 'L0_cond_w_recept': 6.101}
    for name, (base, spread) in spreads.items():
        noise = np.random.default_rng([zlib.crc32(name.encode()), seed]).standard_normal(out[name].shape)
        drawn = base * np.exp(spread * noise) if base else spread * noise
        out[name] = jnp.asarray(drawn.astype(out[name].dtype))
    for name, factor in factors.items():
        out[name] = (out[name] * factor).astype(out[name].dtype)
    return out
```

```python
from contextlib import ExitStack

import concourse.bass as bass
from concourse import mybir

F32 = mybir.dt.float32
F32R = mybir.dt.float32r
BF16 = mybir.dt.bfloat16
I32 = mybir.dt.int32
ALU = mybir.AluOpType
ACT = mybir.ActivationFunctionType
AX_X = mybir.AxisListType.X

HASH_PRIME = 5099
P = 128
RAW_SLOTS = 3
H_SLOTS = 3
MIX_SLOTS = 3


def moe_token_shift(nc, xs, ids, maa_k, maa_r, w_recept, w_key, w_value, out):
    B, T = ids.shape
    E, D, F = w_key.shape
    N = B * T
    C = N // E
    J = N // P
    ST = C // P
    A = N // P
    KD, KF = D // P, F // P
    assert E & (E - 1) == 0 and E * C == N and T & (T - 1) == 0 and T % J == 0
    assert D == 512 and F % P == 0 and ST == KD == 4 and KF == 8
    CHUNK = F
    FPC = CHUNK // D
    NCH = KD + KF // FPC

    with ExitStack() as ctx:
        def sb(name, shape, dt):
            return ctx.enter_context(nc.sbuf_tensor(name, shape, dt))

        def psum(name):
            return ctx.enter_context(nc.psum_tensor(name, [P, 512], F32))

        def sem(name):
            return ctx.enter_context(nc.semaphore(name))

        ident = sb("ident", [P, P], F32)
        maak = sb("maak", [P, KD], F32)
        maar = sb("maar", [P, KD], F32)
        mask = sb("mask", [P, A], F32)
        row_cur = sb("row_cur", [P, A], I32)
        row_prev = sb("row_prev", [P, A], I32)
        row_out = sb("row_out", [P, A], I32)
        wr_hi = sb("wr_hi", [P, KD, D], F32R)
        wr_lo = sb("wr_lo", [P, KD, D], F32R)
        raw = sb("raw", [P, RAW_SLOTS, CHUNK], F32)
        wk_hi = sb("wk_hi", [P, KD, F], F32R)
        wk_lo = sb("wk_lo", [P, KD, F], F32R)
        wv_hi = sb("wv_hi", [P, KF, D], F32R)
        wv_lo = sb("wv_lo", [P, KF, D], F32R)
        xrow = sb("xrow", [P, 2, ST, D], F32)
        dxrow = sb("dxrow", [P, ST, D], F32)
        xT = sb("xT", [P, 2, C], F32)
        mix = sb("mix", [P, MIX_SLOTS, C], F32)
        xk_hi = sb("xk_hi", [P, KD, C], F32R)
        xk_lo = sb("xk_lo", [P, KD, C], F32R)
        xr_hi = sb("xr_hi", [P, KD, C], F32R)
        xr_lo = sb("xr_lo", [P, KD, C], F32R)
        hid = sb("hid", [P, H_SLOTS, C], F32)
        h_hi = sb("h_hi", [P, KF, C], F32R)
        h_lo = sb("h_lo", [P, KF, C], F32R)
        gate = sb("gate", [P, ST, D], F32)

        xflat = xrow[:, :, :, :].rearrange("p a t d -> p (a t d)")
        onehot = xflat[:, 0:E * J].rearrange("p (e j) -> p e j", e=E)
        cum = xflat[:, E * J:2 * E * J].rearrange("p (e j) -> p e j", e=E)
        prod = xflat[:, 2 * E * J:3 * E * J].rearrange("p (e j) -> p e j", e=E)
        keepmask = xflat[:, 3 * E * J:4 * E * J].rearrange("p (e j) -> p e j", e=E)
        small = gate[:, :, :].rearrange("p t d -> p (t d)")
        cursor = [0]

        def scratch(n, dt=F32):
            at = cursor[0]
            cursor[0] += n
            v = small[:, at:at + n]
            return v if dt == F32 else v.bitcast(dt)

        id_i = scratch(J, I32)
        e_i = scratch(J, I32)
        e_f = scratch(J)
        slot_keep = scratch(J)
        within = scratch(J)
        keep = scratch(J)
        drop = scratch(J)
        drop_cum = scratch(J)
        drop_rank = scratch(J)
        slot_drop = scratch(J)
        slot_diff = scratch(J)
        slot_f = scratch(J)
        slot_i = scratch(J, I32)
        b_i = scratch(J, I32)
        a_i = scratch(J, I32)
        b_f = scratch(J)
        a_f = scratch(J)
        iota_e = scratch(E)
        slot_base = scratch(E)
        off = scratch(E)
        filled = scratch(E)
        empty = scratch(E)
        empty_incl = scratch(E)
        empty_excl = scratch(E)
        ones_j = scratch(J)
        lane = scratch(1)
        slot_pos = scratch(ST)
        tok_j = scratch(A)
        tok_f = scratch(A)
        tok_i = scratch(A, I32)
        batch_i = scratch(A, I32)
        batch_f = scratch(A)
        assert cursor[0] <= ST * D
        bfs = dxrow[:, :, :].rearrange("p t d -> p (t d)").bitcast(BF16)
        tri = bfs[:, 512:512 + P]
        ones = bfs[:, 640:640 + P]
        totals = bfs[:, 768:768 + E]
        drop_total = bfs[:, 784:786]
        iota_row = bfs[:, 800:800 + P]
        OHS = 8
        oh_b = mix[:, :, :].rearrange("p s c -> p (s c)").bitcast(BF16)[:, 0:OHS * P].rearrange(
            "p (s b) -> p s b", s=OHS)
        oh_a = hid[:, :, :].rearrange("p s c -> p (s c)").bitcast(BF16)[:, 0:OHS * 2 * A].rearrange(
            "p (s h a) -> p s h a", s=OHS, h=2)

        acc = [psum(f"acc{i}") for i in range(4)]
        tx = [psum(f"tx{i}") for i in range(2)]
        td = [psum(f"td{i}") for i in range(2)]
        count_ps = acc[0]
        drop_ps = acc[1]
        inv_ps = acc[2]

        s_ids = sem("s_ids")
        s_maa = sem("s_maa")
        s_wrec = [sem(f"s_wrec{k}") for k in range(KD)]
        s_raw = [sem(f"s_raw{i}") for i in range(RAW_SLOTS)]
        s_cur = [[sem(f"s_cur{b}{t}") for t in range(ST)] for b in range(2)]
        s_prev = [sem(f"s_prev{t}") for t in range(ST)]
        s_scat = [[sem(f"s_scat{b}{t}") for t in range(ST)] for b in range(2)]
        s_zero = sem("s_zero")
        s_const = sem("s_const")
        s_route = sem("s_route")
        s_count = sem("s_count")
        s_oh = sem("s_oh")
        s_inv = sem("s_inv")
        s_rows = sem("s_rows")
        s_wrT = sem("s_wrT")
        s_wrhi = sem("s_wrhi")
        s_wrlo = sem("s_wrlo")
        s_whi = sem("s_whi")
        s_wlo = sem("s_wlo")
        s_dx = sem("s_dx")
        s_T = sem("s_T")
        s_xT = sem("s_xT")
        s_mix = sem("s_mix")
        s_xhi = sem("s_xhi")
        s_xlo = sem("s_xlo")
        s_R = sem("s_R")
        s_gate = sem("s_gate")
        s_U = sem("s_U")
        s_relu = sem("s_relu")
        s_sq = sem("s_sq")
        s_hhi = sem("s_hhi")
        s_hlo = sem("s_hlo")
        s_D = sem("s_D")
        s_y = sem("s_y")
        s_res = sem("s_res")

        wr_raw = raw[:, 0:2, :].rearrange("p s (h d) -> p (s h) d", d=D)

        block = ctx.enter_context(nc.Block())

        @block.sync
        def _(sp):
            sp.dma_start(id_i, ids.rearrange("b (q j) -> (b q) j", j=J)).then_inc(s_ids, 16)
            for k in range(KD):
                sp.dma_start(wr_raw[:, k, :], w_recept[k * P:(k + 1) * P, :]).then_inc(s_wrec[k], 16)
            with nc.allow_non_contiguous_dma("512 mixing factors, one per partition and chunk"):
                sp.dma_start(maak[:, :], maa_k.rearrange("(k p) -> p k", p=P)).then_inc(s_maa, 16)
                sp.dma_start(maar[:, :], maa_r.rearrange("(k p) -> p k", p=P)).then_inc(s_maa, 16)
            key = w_key.rearrange("e (k p) f -> e k p f", p=P)
            value = w_value.rearrange("e (c i p) d -> e c p i d", p=P, i=FPC)
            for n in range(E * NCH):
                e, c = divmod(n, NCH)
                if n < 2:
                    sp.wait_ge(s_wrT, KD)
                if n >= RAW_SLOTS:
                    sp.wait_ge(s_wlo, n - RAW_SLOTS + 1)
                slot = raw[:, n % RAW_SLOTS, :]
                if c < KD:
                    sp.dma_start(slot, key[e, c]).then_inc(s_raw[n % RAW_SLOTS], 16)
                else:
                    sp.dma_start(slot.rearrange("p (i d) -> p i d", i=FPC),
                                 value[e, c - KD]).then_inc(s_raw[n % RAW_SLOTS], 16)

        @block.gpsimd
        def _(pool):
            pool.memset(ident[:, :], 0.0).then_inc(s_zero, 1)
            pool.memset(tri, 1.0).then_inc(s_zero, 1)
            pool.memset(ones, 1.0).then_inc(s_const, 1)
            pool.memset(ones_j, 1.0).then_inc(s_const, 1)
            pool.memset(keepmask, 1.0).then_inc(s_zero, 1)
            pool.iota(iota_e, [[1, E]], base=0, channel_multiplier=0,
                      allow_small_or_imprecise_dtypes=True).then_inc(s_const, 1)
            pool.iota(slot_base, [[C, E]], base=-1, channel_multiplier=0,
                      allow_small_or_imprecise_dtypes=True).then_inc(s_const, 1)
            pool.iota(iota_row, [[1, P]], base=0, channel_multiplier=0,
                      allow_small_or_imprecise_dtypes=True).then_inc(s_const, 1)
            pool.iota(lane, [[0, 1]], base=0, channel_multiplier=1,
                      allow_small_or_imprecise_dtypes=True).then_inc(s_const, 1)
            pool.iota(slot_pos, [[P, ST]], base=0, channel_multiplier=1,
                      allow_small_or_imprecise_dtypes=True).then_inc(s_const, 1)
            pool.wait_ge(s_zero, 3)
            pool.affine_select(out=ident[:, :], in_=ident[:, :], compare_op=ALU.not_equal, fill=1.0,
                               base=0, pattern=[[-1, P]], channel_multiplier=1).then_inc(s_const, 1)
            pool.affine_select(out=tri, in_=tri, compare_op=ALU.is_gt, fill=0.0,
                               base=0, pattern=[[1, P]], channel_multiplier=-1).then_inc(s_const, 1)
            pool.memset(keepmask[:, :, 0:1], 0.0).then_inc(s_const, 1)

            def gather(e, t, rows, dst, s):
                a = e * ST + t
                pool.indirect_dma_start(dst, None, xs,
                                        bass.IndirectOffsetOnAxis(rows[:, a:a + 1], 0)).then_inc(s, 16)

            def gather_prev(e):
                if e > 0:
                    pool.wait_ge(s_T, KD * e)
                for t in range(ST):
                    gather(e, t, row_prev, dxrow[:, t, :], s_prev[t])

            def gather_cur(e):
                for t in range(ST):
                    if e >= 2:
                        pool.wait_ge(s_scat[e % 2][t], 16 * (e // 2))
                    gather(e, t, row_cur, xrow[:, e % 2, t, :], s_cur[e % 2][t])

            def scatter(e, t):
                a = e * ST + t
                pool.wait_ge(s_res, e * ST + t + 1)
                pool.indirect_dma_start(out, bass.IndirectOffsetOnAxis(row_out[:, a:a + 1], 0),
                                        xrow[:, e % 2, t, :], None).then_inc(s_scat[e % 2][t], 16)

            pool.wait_ge(s_rows, 1)
            gather_prev(0)
            gather_cur(0)
            gather_cur(1)
            gather_prev(1)
            for e in range(E):
                scatter(e, 0)
                scatter(e, 1)
                if e + 2 < E:
                    gather_prev(e + 2)
                scatter(e, 2)
                scatter(e, 3)
                if e + 2 < E:
                    gather_cur(e + 2)
            for b in range(2):
                for t in range(ST):
                    pool.wait_ge(s_scat[b][t], 16 * (E // 2))

        def weight_dst(n, key, value):
            c = n % NCH
            return key[:, c, :] if c < KD else value[:, (c - KD) * FPC:(c - KD + 1) * FPC, :].rearrange(
                "p i d -> p (i d)")

        @block.scalar
        def _(act):
            def split_weight(n):
                e, c = divmod(n, NCH)
                act.wait_ge(s_raw[n % RAW_SLOTS], 16 * (n // RAW_SLOTS + 1))
                if e > 0 and c == 0:
                    act.wait_ge(s_U, KF * e)
                if e > 0 and c == KD:
                    act.wait_ge(s_D, ST * e)
                act.copy(weight_dst(n, wk_hi, wv_hi), raw[:, n % RAW_SLOTS, :]).then_inc(s_whi, 1)

            def copy_xT(e, k):
                n = e * KD + k
                act.wait_ge(s_T, n + 1)
                act.copy(xT[:, n % 2, :], tx[n % 2][:, :]).then_inc(s_xT, 1)

            def split_mix(e, k):
                for i, hi in enumerate((xr_hi, xk_hi)):
                    v = (e * KD + k) * 2 + i
                    act.wait_ge(s_mix, v + 1)
                    act.copy(hi[:, k, :], mix[:, v % MIX_SLOTS, :]).then_inc(s_xhi, 1)

            def relu(n):
                act.wait_ge(s_U, n + 1)
                if n >= H_SLOTS:
                    act.wait_ge(s_hlo, n - H_SLOTS + 1)
                act.activation(hid[:, n % H_SLOTS, :], acc[n % 4][:, :], ACT.Relu).then_inc(s_relu, 1)

            def split_hidden(n):
                act.wait_ge(s_sq, n + 1)
                act.copy(h_hi[:, n % KF, :], hid[:, n % H_SLOTS, :]).then_inc(s_hhi, 1)

            def sigmoid(e, t):
                act.wait_ge(s_R, e * ST + t + 1)
                if e > 0:
                    act.wait_ge(s_res, (e - 1) * ST + t + 1)
                act.activation(gate[:, t, :], acc[t][:, :], ACT.Sigmoid).then_inc(s_gate, 1)

            for k in range(KD):
                act.wait_ge(s_wrT, k + 1)
                act.copy(wr_hi[:, k, :], (tx[0], td[0], tx[1], td[1])[k][:, :]).then_inc(s_wrhi, 1)
            for c in range(RAW_SLOTS):
                split_weight(c)

            def mixes(e, weights):
                copy_xT(e, 0)
                copy_xT(e, 1)
                split_mix(e, 0)
                split_mix(e, 1)
                for k in (2, 3):
                    if weights:
                        split_weight(weights.pop(0))
                    copy_xT(e, k)
                    split_mix(e, k)
                for n in weights:
                    split_weight(n)
                for t in range(ST):
                    sigmoid(e, t)

            mixes(0, [RAW_SLOTS])
            for e in range(E):
                for m in range(KF):
                    n = e * KF + m
                    relu(n)
                    if m > 0:
                        split_hidden(n - 1)
                    if m < NCH - KD:
                        split_weight(e * NCH + KD + m)
                split_hidden(n)
                if e + 1 < E:
                    mixes(e + 1, [(e + 1) * NCH + c for c in range(KD)])

        @block.vector
        def _(dve):
            steps = [0]

            def step(ins):
                steps[0] += 1
                ins.then_inc(s_route, 1)
                dve.wait_ge(s_route, steps[0])

            def over_j(v):
                return v.unsqueeze(2).to_broadcast([P, E, J])

            def over_e(v):
                return v.unsqueeze(1).to_broadcast([P, E, J])

            dve.wait_ge(s_ids, 16)
            step(dve.tensor_scalar(e_i, id_i, E - 1, None, ALU.bitwise_and))
            step(dve.tensor_scalar(e_i, e_i, HASH_PRIME % E, None, ALU.mult))
            step(dve.tensor_scalar(e_i, e_i, E - 1, None, ALU.bitwise_and))
            step(dve.tensor_copy(e_f, e_i))
            dve.wait_ge(s_const, 10)
            step(dve.tensor_tensor(onehot, over_e(e_f), over_j(iota_e), ALU.is_equal))
            step(dve.tensor_tensor_scan(cum.rearrange("p e j -> p (e j)"),
                                        keepmask.rearrange("p e j -> p (e j)"),
                                        onehot.rearrange("p e j -> p (e j)"), 0.0, ALU.mult, ALU.add))
            step(dve.tensor_copy(totals, cum[:, :, J - 1]))
            dve.wait_ge(s_count, 1)
            step(dve.tensor_tensor(off, count_ps[:, 0:E], slot_base, ALU.add))
            step(dve.tensor_tensor(cum, cum, over_j(off), ALU.add))
            step(dve.tensor_tensor(prod, cum, onehot, ALU.mult))
            step(dve.tensor_reduce(slot_keep, prod.rearrange("p e j -> p j e"), AX_X, ALU.add))
            step(dve.scalar_tensor_tensor(within, e_f, -float(C), slot_keep, ALU.mult, ALU.add))
            step(dve.tensor_scalar(keep, within, float(C), None, ALU.is_lt))
            step(dve.tensor_scalar(drop, within, float(C), None, ALU.is_ge))
            step(dve.tensor_tensor_scan(drop_cum, ones_j, drop, 0.0, ALU.mult, ALU.add))
            step(dve.tensor_copy(drop_total[:, 0:1], drop_cum[:, J - 1:J]))
            step(dve.tensor_scalar(filled, count_ps[:, E:2 * E], float(C), None, ALU.min))
            step(dve.tensor_scalar(empty, filled, -1.0, float(C), ALU.mult, ALU.add))
            step(dve.tensor_tensor_scan(empty_incl, ones_j[:, 0:E], empty, 0.0, ALU.mult, ALU.add))
            step(dve.tensor_tensor(empty_excl, empty_incl, empty, ALU.subtract))
            dve.wait_ge(s_count, 2)
            step(dve.tensor_scalar(drop_rank, drop_cum, drop_ps[:, 0:1], -1.0, ALU.add, ALU.add))
            step(dve.tensor_tensor(prod, over_e(drop_rank), over_j(empty_excl), ALU.is_ge))
            step(dve.tensor_tensor(prod, prod, over_j(filled), ALU.mult))
            step(dve.tensor_reduce(slot_drop, prod.rearrange("p e j -> p j e"), AX_X, ALU.add))
            step(dve.tensor_tensor(slot_drop, slot_drop, drop_rank, ALU.add))
            step(dve.tensor_tensor(slot_diff, slot_keep, slot_drop, ALU.subtract))
            step(dve.tensor_tensor(slot_diff, slot_diff, keep, ALU.mult))
            step(dve.tensor_tensor(slot_f, slot_diff, slot_drop, ALU.add))
            step(dve.tensor_copy(slot_i, slot_f))
            step(dve.tensor_scalar(b_i, slot_i, P - 1, None, ALU.bitwise_and))
            step(dve.tensor_scalar(a_i, slot_i, P.bit_length() - 1, None, ALU.logical_shift_right))
            step(dve.tensor_copy(b_f, b_i))
            step(dve.tensor_copy(a_f, a_i))
            for j in range(J):
                if j >= OHS:
                    dve.wait_ge(s_inv, j - OHS + 1)
                dve.tensor_scalar(oh_b[:, j % OHS, :], iota_row, b_f[:, j:j + 1], None, ALU.is_equal)
                dve.tensor_scalar(oh_a[:, j % OHS, 0, :], iota_row[:, 0:A], a_f[:, j:j + 1], lane,
                                  ALU.is_equal, ALU.mult)
                dve.tensor_scalar(oh_a[:, j % OHS, 1, :], iota_row[:, 0:A], a_f[:, j:j + 1], float(j),
                                  ALU.is_equal, ALU.mult).then_inc(s_oh, 1)
            dve.wait_ge(s_inv, J)
            step(dve.tensor_copy(tok_j, inv_ps[:, A:2 * A]))
            step(dve.scalar_tensor_tensor(tok_f, inv_ps[:, 0:A], float(J), tok_j, ALU.mult, ALU.add))
            step(dve.tensor_copy(tok_i, tok_f))
            step(dve.tensor_scalar(batch_i, tok_i, T.bit_length() - 1, None, ALU.logical_shift_right))
            step(dve.tensor_copy(batch_f, batch_i))
            step(dve.tensor_copy(row_out[:, :], tok_i))
            step(dve.tensor_tensor(row_prev[:, :], tok_f, batch_f, ALU.add))
            step(dve.scalar_tensor_tensor(row_cur[:, :], tok_f, 1.0, batch_f, ALU.add, ALU.add))
            dve.tensor_tensor(mask[:, :].rearrange("p (e t) -> p e t", t=ST),
                              slot_pos.unsqueeze(1).to_broadcast([P, E, ST]),
                              filled.unsqueeze(2).to_broadcast([P, E, ST]), ALU.is_lt).then_inc(s_rows, 1)

            for k in range(KD):
                dve.wait_ge(s_wrhi, k + 1)
                dve.tensor_tensor(wr_lo[:, k, :], (tx[0], td[0], tx[1], td[1])[k][:, :],
                                  wr_hi[:, k, :].bitcast(F32), ALU.subtract).then_inc(s_wrlo, 1)

            def split_weight(n):
                dve.wait_ge(s_whi, n + 1)
                dve.tensor_tensor(weight_dst(n, wk_lo, wv_lo), raw[:, n % RAW_SLOTS, :],
                                  weight_dst(n, wk_hi, wv_hi).bitcast(F32), ALU.subtract).then_inc(s_wlo, 1)

            def diff(e, t):
                dve.wait_ge(s_prev[t], 16 * (e + 1))
                dve.wait_ge(s_cur[e % 2][t], 16 * (e // 2 + 1))
                dve.tensor_tensor(dxrow[:, t, :], dxrow[:, t, :], xrow[:, e % 2, t, :],
                                  ALU.subtract).then_inc(s_dx, 1)

            def mix_sum(e, k, i):
                n = e * KD + k
                v = 2 * n + i
                if i == 0:
                    dve.wait_ge(s_xT, n + 1)
                if v >= MIX_SLOTS:
                    dve.wait_ge(s_xlo, v - MIX_SLOTS + 1)
                dve.scalar_tensor_tensor(mix[:, v % MIX_SLOTS, :], td[n % 2][:, :],
                                         (maar, maak)[i][:, k:k + 1], xT[:, n % 2, :],
                                         ALU.mult, ALU.add).then_inc(s_mix, 1)

            def split_mix(e, k, i):
                v = (e * KD + k) * 2 + i
                dve.wait_ge(s_xhi, v + 1)
                dve.tensor_tensor((xr_lo, xk_lo)[i][:, k, :], mix[:, v % MIX_SLOTS, :],
                                  (xr_hi, xk_hi)[i][:, k, :].bitcast(F32), ALU.subtract).then_inc(s_xlo, 1)

            def square(n):
                dve.wait_ge(s_relu, n + 1)
                h = hid[:, n % H_SLOTS, :]
                dve.tensor_tensor(h, h, h, ALU.mult).then_inc(s_sq, 1)

            def split_hidden(n):
                dve.wait_ge(s_hhi, n + 1)
                dve.tensor_tensor(h_lo[:, n % KF, :], hid[:, n % H_SLOTS, :],
                                  h_hi[:, n % KF, :].bitcast(F32), ALU.subtract).then_inc(s_hlo, 1)

            def result(e, t):
                n = e * ST + t
                dve.wait_ge(s_D, n + 1)
                dve.scalar_tensor_tensor(gate[:, t, :], acc[t][:, :], mask[:, n:n + 1], gate[:, t, :],
                                         ALU.mult, ALU.mult).then_inc(s_y, 1)
                dve.wait_ge(s_y, n + 1)
                dve.tensor_tensor(xrow[:, e % 2, t, :], gate[:, t, :], xrow[:, e % 2, t, :],
                                  ALU.add).then_inc(s_res, 1)

            def mixes(e, between):
                mix_sum(e, 0, 0)
                mix_sum(e, 0, 1)
                mix_sum(e, 1, 0)
                split_mix(e, 0, 0)
                mix_sum(e, 1, 1)
                split_mix(e, 0, 1)
                split_mix(e, 1, 0)
                split_mix(e, 1, 1)
                between[0]()
                for k in (2, 3):
                    mix_sum(e, k, 0)
                    mix_sum(e, k, 1)
                    split_mix(e, k, 0)
                    split_mix(e, k, 1)
                    between[k - 1]()

            for c in range(RAW_SLOTS):
                split_weight(c)
            for t in range(ST):
                diff(0, t)
            dve.wait_ge(s_maa, 32)
            mixes(0, [lambda: split_weight(RAW_SLOTS), lambda: None, lambda: None])
            for e in range(E):
                for m in range(KF):
                    n = e * KF + m
                    square(n)
                    if m > 0:
                        split_hidden(n - 1)
                    if m < NCH - KD:
                        split_weight(e * NCH + KD + m)
                    elif e + 1 < E:
                        diff(e + 1, m - (NCH - KD))
                split_hidden(n)
                if e + 1 == E:
                    for t in range(ST):
                        result(e, t)
                    continue
                w = (e + 1) * NCH

                def after_pair():
                    split_weight(w)
                    result(e, 0)

                def after_2():
                    split_weight(w + 1)
                    result(e, 1)

                def after_3():
                    split_weight(w + 2)
                    result(e, 2)
                    split_weight(w + 3)
                    result(e, 3)

                mixes(e + 1, [after_pair, after_2, after_3])

        @block.tensor
        def _(pe):
            def transpose_w_recept():
                for k in range(KD):
                    bank = (tx[0], td[0], tx[1], td[1])[k]
                    for r in range(KD):
                        if k == 0:
                            pe.wait_ge(s_wrec[r], 16)
                        last = pe.transpose(bank[:, r * P:(r + 1) * P], wr_raw[:, r, k * P:(k + 1) * P],
                                            ident[:, :])
                    last.then_inc(s_wrT, 1)

            def transposes(e, k):
                n = e * KD + k
                if n >= 2:
                    pe.wait_ge(s_mix, 2 * (n - 1))
                for t in range(ST):
                    if k == 0:
                        pe.wait_ge(s_dx, e * ST + t + 1)
                    pe.transpose(tx[n % 2][:, t * P:(t + 1) * P], xrow[:, e % 2, t, k * P:(k + 1) * P],
                                 ident[:, :])
                    last = pe.transpose(td[n % 2][:, t * P:(t + 1) * P], dxrow[:, t, k * P:(k + 1) * P],
                                        ident[:, :])
                last.then_inc(s_T, 1)

            def triple(bank, hi, lo, m_hi, m_lo, first, last):
                pe.matmul(bank[:, :], hi, m_hi, start=first, stop=False)
                pe.matmul(bank[:, :], hi, m_lo, start=False, stop=False)
                return pe.matmul(bank[:, :], lo, m_hi, start=False, stop=last)

            def receptance(e, t):
                if e > 0:
                    pe.wait_ge(s_y, (e - 1) * ST + t + 1)
                for k in range(KD):
                    if t == 0:
                        pe.wait_ge(s_xlo, (e * KD + k) * 2 + 1)
                    rows = slice(t * P, (t + 1) * P)
                    mm = triple(acc[t], xr_hi[:, k, rows], xr_lo[:, k, rows], wr_hi[:, k, :], wr_lo[:, k, :],
                                k == 0, k == KD - 1)
                mm.then_inc(s_R, 1)

            def up(e, m):
                n = e * KF + m
                if m < ST:
                    pe.wait_ge(s_gate, e * ST + m + 1)
                else:
                    pe.wait_ge(s_relu, n - 3)
                cols = slice(m * P, (m + 1) * P)
                for k in range(KD):
                    if m == 0:
                        pe.wait_ge(s_wlo, e * NCH + k + 1)
                        pe.wait_ge(s_xlo, (e * KD + k) * 2 + 2)
                    mm = triple(acc[m % 4], wk_hi[:, k, cols], wk_lo[:, k, cols], xk_hi[:, k, :],
                                xk_lo[:, k, :], k == 0, k == KD - 1)
                mm.then_inc(s_U, 1)

            def down(e, t):
                pe.wait_ge(s_relu, e * KF + 5 + t)
                rows = slice(t * P, (t + 1) * P)
                for k in range(KF):
                    if t == 0:
                        if k % FPC == 0:
                            pe.wait_ge(s_wlo, e * NCH + KD + k // FPC + 1)
                        pe.wait_ge(s_hlo, e * KF + k + 1)
                    mm = triple(acc[t], h_hi[:, k, rows], h_lo[:, k, rows], wv_hi[:, k, :], wv_lo[:, k, :],
                                k == 0, k == KF - 1)
                mm.then_inc(s_D, 1)

            pe.wait_ge(s_const, 10)
            transpose_w_recept()
            pe.wait_ge(s_route, 7)
            pe.matmul(count_ps[:, 0:E], tri, totals, start=True, stop=True)
            pe.matmul(count_ps[:, E:2 * E], ones, totals, start=True, stop=True).then_inc(s_count, 1)
            pe.wait_ge(s_route, 16)
            pe.matmul(drop_ps[:, 0:1], tri, drop_total[:, 0:1], start=True, stop=True).then_inc(s_count, 1)
            for j in range(J):
                pe.wait_ge(s_oh, j + 1)
                pe.matmul(inv_ps[:, 0:2 * A], oh_b[:, j % OHS, :],
                          oh_a[:, j % OHS, :, :].rearrange("p h a -> p (h a)"),
                          start=(j == 0), stop=(j == J - 1)).then_inc(s_inv, 1)

            pe.wait_ge(s_wrlo, KD)
            for k in range(KD):
                transposes(0, k)
            for t in range(ST):
                receptance(0, t)
            for e in range(E):
                for m in range(KF):
                    up(e, m)
                more = e + 1 < E
                if more:
                    transposes(e + 1, 0)
                    transposes(e + 1, 1)
                for t in range(ST):
                    down(e, t)
                    if more and t < 2:
                        transposes(e + 1, 2 + t)
                if more:
                    for t in range(ST):
                        receptance(e + 1, t)


def kernel(**inputs):
    import numpy as _np
    import concourse.bacc as _bacc
    from concourse import mybir as _mybir
    from concourse.bass_utils import run_bass_kernel_spmd as _run

    x = _np.asarray(inputs["x"])
    cond = _np.asarray(inputs["cond_1024"])
    B, T, D = x.shape
    arrays = {
        "xs": _np.concatenate([cond[:, None, :], x], axis=1).reshape(B * (T + 1), D),
        "token_ids": _np.ascontiguousarray(inputs["itok_BxS_2_50255"]),
        "time_maa_k": _np.ascontiguousarray(inputs["L0_cond_time_maa_k"]),
        "time_maa_r": _np.ascontiguousarray(inputs["L0_cond_time_maa_r"]),
        "w_recept": _np.ascontiguousarray(inputs["L0_cond_w_recept"]),
        "w_key": _np.ascontiguousarray(inputs["L0_cond_w_key"]),
        "w_value": _np.ascontiguousarray(inputs["L0_cond_w_value"]),
    }
    nc = _bacc.Bacc("TRN2", target_bir_lowering=False, num_devices=1)
    args = [nc.dram_tensor(name, a.shape, _mybir.dt.from_np(a.dtype), kind="ExternalInput").ap()
            for name, a in arrays.items()]
    out = nc.dram_tensor("out", (B * T, D), _mybir.dt.float32, kind="ExternalOutput").ap()
    moe_token_shift(nc, *args, out)
    r = _run(nc, [arrays], core_ids=[0])
    return r.results[0]["out"].reshape(B, T, D)
```

```python
from contextlib import ExitStack

import concourse.bass as bass
from concourse import mybir

F32 = mybir.dt.float32
F32R = mybir.dt.float32r
BF16 = mybir.dt.bfloat16
I32 = mybir.dt.int32
ALU = mybir.AluOpType
ACT = mybir.ActivationFunctionType
AX_X = mybir.AxisListType.X

HASH_PRIME = 5099
P = 128
RAW_SLOTS = 3
H_SLOTS = 3
MIX_SLOTS = 3


def moe_token_shift(nc, xs, ids, maa_k, maa_r, w_recept, w_key, w_value, out):
    B, T = ids.shape
    E, D, F = w_key.shape
    N = B * T
    C = N // E
    J = N // P
    ST = C // P
    A = N // P
    KD, KF = D // P, F // P
    assert E & (E - 1) == 0 and E * C == N and T & (T - 1) == 0 and T % J == 0
    assert D == 512 and F == 2 * D and ST == KD == 4 and KF == 8
    unhash = pow(HASH_PRIME, -1, E)
    CHUNK = F
    FPC = CHUNK // D
    NCH = KD + KF // FPC
    N_CONST = 7
    ROUTE_TOTALS, ROUTE_DROPS = 7, 22

    with ExitStack() as ctx:
        def sb(name, shape, dt):
            return ctx.enter_context(nc.sbuf_tensor(name, shape, dt))

        def psum(name):
            return ctx.enter_context(nc.psum_tensor(name, [P, 512], F32))

        def sem(name):
            return ctx.enter_context(nc.semaphore(name))

        ident = sb("ident", [P, P], F32)
        maak = sb("maak", [P, KD], F32)
        maar = sb("maar", [P, KD], F32)
        mask = sb("mask", [P, A], F32)
        row_cur = sb("row_cur", [P, A], I32)
        row_prev = sb("row_prev", [P, A], I32)
        row_out = sb("row_out", [P, A], I32)
        wr_hi = sb("wr_hi", [P, KD, D], F32R)
        wr_lo = sb("wr_lo", [P, KD, D], F32R)
        raw = sb("raw", [P, RAW_SLOTS, CHUNK], F32)
        wk_hi = sb("wk_hi", [P, KD, F], F32R)
        wk_lo = sb("wk_lo", [P, KD, F], F32R)
        xrow = sb("xrow", [P, 2, ST, D], F32)
        dxrow = sb("dxrow", [P, ST, D], F32)

        with ExitStack() as routing:
            def rt(name, shape, dt=F32):
                return routing.enter_context(nc.sbuf_tensor(name, shape, dt))

            residue = rt("residue", [P, E], I32)
            residue_b = rt("residue_b", [P, E], BF16)
            segment = rt("segment", [P, E, J], BF16)
            onehot = rt("onehot", [P, E, J], BF16)
            cum = rt("cum", [P, E, J])
            prod = rt("prod", [P, E, J])
            tri = rt("tri", [P, P], BF16)
            ones = rt("ones", [P, P], BF16)
            totals = rt("totals", [P, E], BF16)
            drop_total = rt("drop_total", [P, 1], BF16)
            index_b = rt("index_b", [P, P, J], BF16)
            index_j = rt("index_j", [P, J], BF16)
            oh_b = rt("oh_b", [P, P, J], BF16)
            oh_a = rt("oh_a", [P, A, J], BF16)
            oh_aw = rt("oh_aw", [P, 2, A, J], BF16)
            b_b = rt("b_b", [P, J], BF16)
            a_b = rt("a_b", [P, J], BF16)
            wide = {name: rt(name, [P, J], dt) for name, dt in (
                ("id_i", I32), ("id_low", I32), ("id_low_b", BF16), ("e_i", I32), ("e_f", F32),
                ("slot_keep", F32), ("within", F32), ("keep", F32), ("drop", F32), ("drop_cum", F32),
                ("drop_rank", F32), ("slot_drop", F32), ("slot_diff", F32), ("slot_i", I32),
                ("b_i", I32), ("a_i", I32), ("ones_j", F32))}
            slot_base = rt("slot_base", [P, E])
            off = rt("off", [P, E])
            filled = rt("filled", [P, E])
            empty = rt("empty", [P, E])
            empty_incl = rt("empty_incl", [P, E])
            empty_excl = rt("empty_excl", [P, E])
            lane = rt("lane", [P, 1])
            slot_pos = rt("slot_pos", [P, ST])
            tok_j = rt("tok_j", [P, A])
            tok_f = rt("tok_f", [P, A])
            tok_i = rt("tok_i", [P, A], I32)
            batch_i = rt("batch_i", [P, A], I32)
            batch_f = rt("batch_f", [P, A])
        id_i = wide["id_i"][:, :]

        wv_hi = sb("wv_hi", [P, KF, D], F32R)
        wv_lo = sb("wv_lo", [P, KF, D], F32R)
        xT = sb("xT", [P, 2, C], F32)
        mix = sb("mix", [P, MIX_SLOTS, C], F32)
        xk_hi = sb("xk_hi", [P, KD, C], F32R)
        xk_lo = sb("xk_lo", [P, KD, C], F32R)
        xr_hi = sb("xr_hi", [P, KD, C], F32R)
        xr_lo = sb("xr_lo", [P, KD, C], F32R)
        hid = sb("hid", [P, H_SLOTS, C], F32)
        h_hi = sb("h_hi", [P, KF, C], F32R)
        h_lo = sb("h_lo", [P, KF, C], F32R)
        gate = sb("gate", [P, ST, D], F32)

        acc = [psum(f"acc{i}") for i in range(4)]
        tx = [psum(f"tx{i}") for i in range(2)]
        td = [psum(f"td{i}") for i in range(2)]
        count_ps = acc[0]
        drop_ps = acc[1]
        inv_ps = (acc[2], acc[3])

        s_ids = sem("s_ids")
        s_maa = sem("s_maa")
        s_wrec = [sem(f"s_wrec{k}") for k in range(KD)]
        s_raw = [sem(f"s_raw{i}") for i in range(RAW_SLOTS)]
        s_cur = [[sem(f"s_cur{b}{t}") for t in range(ST)] for b in range(2)]
        s_prev = [sem(f"s_prev{t}") for t in range(ST)]
        s_scat = [[sem(f"s_scat{b}{t}") for t in range(ST)] for b in range(2)]
        s_zero = sem("s_zero")
        s_table = sem("s_table")
        s_const = sem("s_const")
        s_index = sem("s_index")
        s_route = sem("s_route")
        s_count = sem("s_count")
        s_oh = sem("s_oh")
        s_inv = sem("s_inv")
        s_rows = sem("s_rows")
        s_wrT = sem("s_wrT")
        s_wrhi = sem("s_wrhi")
        s_wrlo = sem("s_wrlo")
        s_whi = sem("s_whi")
        s_wlo = sem("s_wlo")
        s_dx = sem("s_dx")
        s_T = sem("s_T")
        s_xT = sem("s_xT")
        s_mix = sem("s_mix")
        s_xhi = sem("s_xhi")
        s_xlo = sem("s_xlo")
        s_R = sem("s_R")
        s_gate = sem("s_gate")
        s_U = sem("s_U")
        s_relu = sem("s_relu")
        s_sq = sem("s_sq")
        s_hhi = sem("s_hhi")
        s_hlo = sem("s_hlo")
        s_D = sem("s_D")
        s_y = sem("s_y")
        s_res = sem("s_res")

        wr_raw = raw[:, 0:2, :].rearrange("p s (h d) -> p (s h) d", d=D)

        block = ctx.enter_context(nc.Block())

        @block.sync
        def _(sp):
            sp.dma_start(id_i, ids.rearrange("b (q j) -> (b q) j", j=J)).then_inc(s_ids, 16)
            for k in range(KD):
                sp.dma_start(wr_raw[:, k, :], w_recept[k * P:(k + 1) * P, :]).then_inc(s_wrec[k], 16)
            with nc.allow_non_contiguous_dma("512 mixing factors, one per partition and chunk"):
                sp.dma_start(maak[:, :], maa_k.rearrange("(k p) -> p k", p=P)).then_inc(s_maa, 16)
                sp.dma_start(maar[:, :], maa_r.rearrange("(k p) -> p k", p=P)).then_inc(s_maa, 16)
            key = w_key.rearrange("e (k p) f -> e k p f", p=P)
            value = w_value.rearrange("e (c i p) d -> e c p i d", p=P, i=FPC)
            for n in range(E * NCH):
                e, c = divmod(n, NCH)
                if n < 2:
                    sp.wait_ge(s_wrT, KD)
                if n >= RAW_SLOTS:
                    sp.wait_ge(s_wlo, n - RAW_SLOTS + 1)
                slot = raw[:, n % RAW_SLOTS, :]
                if c < KD:
                    sp.dma_start(slot, key[e, c]).then_inc(s_raw[n % RAW_SLOTS], 16)
                else:
                    sp.dma_start(slot.rearrange("p (i d) -> p i d", i=FPC),
                                 value[e, c - KD]).then_inc(s_raw[n % RAW_SLOTS], 16)

        @block.gpsimd
        def _(pool):
            small_ints = {"allow_small_or_imprecise_dtypes": True}
            pool.iota(residue[:, :], [[unhash, E]], base=0, channel_multiplier=0).then_inc(s_table, 1)
            pool.memset(segment[:, :, :], 1.0).then_inc(s_zero, 1)
            pool.wait_ge(s_zero, 1)
            pool.memset(segment[:, :, 0:1], 0.0).then_inc(s_table, 1)
            pool.memset(tri[:, :], 1.0).then_inc(s_zero, 1)
            pool.memset(ones[:, :], 1.0).then_inc(s_const, 1)
            pool.memset(ident[:, :], 0.0).then_inc(s_zero, 1)
            pool.wait_ge(s_zero, 2)
            pool.affine_select(out=tri[:, :], in_=tri[:, :], compare_op=ALU.is_gt, fill=0.0,
                               base=0, pattern=[[1, P]], channel_multiplier=-1).then_inc(s_const, 1)
            pool.iota(slot_base[:, :], [[C, E]], base=-1, channel_multiplier=0,
                      **small_ints).then_inc(s_const, 1)
            pool.memset(wide["ones_j"][:, :], 1.0).then_inc(s_const, 1)
            pool.iota(lane[:, :], [[0, 1]], base=0, channel_multiplier=1,
                      **small_ints).then_inc(s_const, 1)
            pool.iota(slot_pos[:, :], [[P, ST]], base=0, channel_multiplier=1,
                      **small_ints).then_inc(s_const, 1)
            pool.wait_ge(s_zero, 3)
            pool.affine_select(out=ident[:, :], in_=ident[:, :], compare_op=ALU.not_equal, fill=1.0,
                               base=0, pattern=[[-1, P]], channel_multiplier=1).then_inc(s_const, 1)
            pool.iota(index_j[:, :], [[1, J]], base=0, channel_multiplier=0,
                      **small_ints).then_inc(s_index, 1)
            pool.iota(index_b[:, :, :], [[1, P], [0, J]], base=0, channel_multiplier=0,
                      **small_ints).then_inc(s_index, 1)

            def gather(e, t, rows, dst, s):
                a = e * ST + t
                pool.indirect_dma_start(dst, None, xs,
                                        bass.IndirectOffsetOnAxis(rows[:, a:a + 1], 0)).then_inc(s, 16)

            def gather_prev(e, t):
                if e > 0:
                    pool.wait_ge(s_T, KD * e)
                gather(e, t, row_prev, dxrow[:, t, :], s_prev[t])

            def gather_cur(e, t):
                if e >= 2:
                    pool.wait_ge(s_scat[e % 2][t], 16 * (e // 2))
                gather(e, t, row_cur, xrow[:, e % 2, t, :], s_cur[e % 2][t])

            def scatter(e, t):
                a = e * ST + t
                pool.wait_ge(s_res, e * ST + t + 1)
                pool.indirect_dma_start(out, bass.IndirectOffsetOnAxis(row_out[:, a:a + 1], 0),
                                        xrow[:, e % 2, t, :], None).then_inc(s_scat[e % 2][t], 16)

            pool.wait_ge(s_rows, 1)
            for t in range(ST):
                gather_cur(0, t)
                gather_prev(0, t)
            pool.wait_ge(s_rows, 2)
            for t in range(ST):
                gather_cur(1, t)
            for t in range(ST):
                gather_prev(1, t)
            for e in range(E):
                more = e + 2 < E
                scatter(e, 0)
                scatter(e, 1)
                scatter(e, 2)
                if more:
                    for t in range(ST):
                        gather_prev(e + 2, t)
                scatter(e, 3)
                if more:
                    for t in range(ST):
                        gather_cur(e + 2, t)
            for b in range(2):
                for t in range(ST):
                    pool.wait_ge(s_scat[b][t], 16 * (E // 2))

        def weight_dst(n, key, value):
            c = n % NCH
            return key[:, c, :] if c < KD else value[:, (c - KD) * FPC:(c - KD + 1) * FPC, :].rearrange(
                "p i d -> p (i d)")

        @block.scalar
        def _(act):
            def split_weight(n):
                e, c = divmod(n, NCH)
                act.wait_ge(s_raw[n % RAW_SLOTS], 16 * (n // RAW_SLOTS + 1))
                if e > 0 and c == 0:
                    act.wait_ge(s_U, KF * e)
                if e > 0 and c == KD:
                    act.wait_ge(s_D, ST * e)
                act.copy(weight_dst(n, wk_hi, wv_hi), raw[:, n % RAW_SLOTS, :]).then_inc(s_whi, 1)

            def copy_xT(e, k):
                n = e * KD + k
                act.wait_ge(s_T, n + 1)
                act.copy(xT[:, n % 2, :], tx[n % 2][:, :]).then_inc(s_xT, 1)

            def split_mix(e, k):
                for i, hi in enumerate((xr_hi, xk_hi)):
                    v = (e * KD + k) * 2 + i
                    act.wait_ge(s_mix, v + 1)
                    act.copy(hi[:, k, :], mix[:, v % MIX_SLOTS, :]).then_inc(s_xhi, 1)

            def relu(n):
                act.wait_ge(s_U, n + 1)
                if n >= H_SLOTS:
                    act.wait_ge(s_hlo, n - H_SLOTS + 1)
                act.activation(hid[:, n % H_SLOTS, :], acc[n % 4][:, :], ACT.Relu).then_inc(s_relu, 1)

            def split_hidden(n):
                act.wait_ge(s_sq, n + 1)
                act.copy(h_hi[:, n % KF, :], hid[:, n % H_SLOTS, :]).then_inc(s_hhi, 1)

            def sigmoid(e, t):
                act.wait_ge(s_R, e * ST + t + 1)
                if e > 0:
                    act.wait_ge(s_res, (e - 1) * ST + t + 1)
                act.activation(gate[:, t, :], acc[t][:, :], ACT.Sigmoid).then_inc(s_gate, 1)

            for k in range(KD):
                act.wait_ge(s_wrT, k + 1)
                act.copy(wr_hi[:, k, :], (tx[0], td[0], tx[1], td[1])[k][:, :]).then_inc(s_wrhi, 1)

            def mixes(e, weights):
                copy_xT(e, 0)
                copy_xT(e, 1)
                split_mix(e, 0)
                split_mix(e, 1)
                for k in (2, 3):
                    for c in weights[:1]:
                        split_weight(e * NCH + c)
                    weights = weights[1:]
                    copy_xT(e, k)
                    split_mix(e, k)
                for c in weights:
                    split_weight(e * NCH + c)
                for t in range(ST):
                    sigmoid(e, t)

            for c in range(RAW_SLOTS):
                split_weight(c)
            mixes(0, list(range(RAW_SLOTS, KD)))
            for e in range(E):
                for m in range(KF):
                    n = e * KF + m
                    relu(n)
                    if m > 0:
                        split_hidden(n - 1)
                    if m < NCH - KD:
                        split_weight(e * NCH + KD + m)
                split_hidden(n)
                if e + 1 < E:
                    mixes(e + 1, list(range(KD)))

        @block.vector
        def _(dve):
            steps = [0]
            v = {name: t[:, :] for name, t in wide.items()}

            def step(ins, read_next=True):
                steps[0] += 1
                ins.then_inc(s_route, 1)
                if read_next:
                    dve.wait_ge(s_route, steps[0])

            def over_j(w):
                return w[:, :].unsqueeze(2).to_broadcast([P, w.shape[1], J])

            def over(w, n):
                return w.unsqueeze(1).to_broadcast([P, n, J])

            dve.wait_ge(s_table, 1)
            step(dve.tensor_scalar(residue[:, :], residue[:, :], E - 1, None, ALU.bitwise_and))
            step(dve.tensor_copy(residue_b[:, :], residue[:, :]), False)
            dve.wait_ge(s_ids, 16)
            step(dve.tensor_scalar(v["id_low"], v["id_i"], E - 1, None, ALU.bitwise_and))
            step(dve.tensor_copy(v["id_low_b"], v["id_low"]))
            step(dve.tensor_tensor(onehot[:, :, :], over(v["id_low_b"], E), over_j(residue_b),
                                   ALU.is_equal))
            dve.wait_ge(s_table, 2)
            step(dve.tensor_tensor_scan(cum[:, :, :].rearrange("p e j -> p (e j)"),
                                        segment[:, :, :].rearrange("p e j -> p (e j)"),
                                        onehot[:, :, :].rearrange("p e j -> p (e j)"), 0.0,
                                        ALU.mult, ALU.add))
            step(dve.tensor_copy(totals[:, :], cum[:, :, J - 1]), False)
            assert steps[0] == ROUTE_TOTALS
            step(dve.tensor_scalar(v["e_i"], v["id_low"], HASH_PRIME % E, None, ALU.mult))
            step(dve.tensor_scalar(v["e_i"], v["e_i"], E - 1, None, ALU.bitwise_and))
            step(dve.tensor_copy(v["e_f"], v["e_i"]), False)
            dve.wait_ge(s_const, N_CONST)
            dve.wait_ge(s_count, 1)
            step(dve.tensor_tensor(off[:, :], count_ps[:, 0:E], slot_base[:, :], ALU.add), False)
            step(dve.tensor_scalar(filled[:, :], count_ps[:, E:2 * E], float(C), None, ALU.min))
            step(dve.tensor_tensor(cum[:, :, :], cum[:, :, :], over_j(off), ALU.add), False)
            step(dve.tensor_scalar(empty[:, :], filled[:, :], -1.0, float(C), ALU.mult, ALU.add))
            step(dve.tensor_tensor(prod[:, :, :], cum[:, :, :], onehot[:, :, :], ALU.mult), False)
            step(dve.tensor_tensor_scan(empty_incl[:, :], v["ones_j"][:, 0:E], empty[:, :], 0.0,
                                        ALU.mult, ALU.add))
            step(dve.tensor_reduce(v["slot_keep"], prod[:, :, :].rearrange("p e j -> p j e"), AX_X,
                                   ALU.add), False)
            step(dve.tensor_tensor(empty_excl[:, :], empty_incl[:, :], empty[:, :], ALU.subtract))
            step(dve.scalar_tensor_tensor(v["within"], v["e_f"], -float(C), v["slot_keep"],
                                          ALU.mult, ALU.add))
            step(dve.tensor_scalar(v["drop"], v["within"], float(C), None, ALU.is_ge))
            step(dve.tensor_tensor_scan(v["drop_cum"], v["ones_j"], v["drop"], 0.0, ALU.mult, ALU.add))
            step(dve.tensor_copy(drop_total[:, :], v["drop_cum"][:, J - 1:J]), False)
            assert steps[0] == ROUTE_DROPS
            step(dve.tensor_scalar(v["keep"], v["within"], float(C), None, ALU.is_lt), False)
            dve.wait_ge(s_count, 2)
            step(dve.tensor_scalar(v["drop_rank"], v["drop_cum"], drop_ps[:, 0:1], -1.0,
                                   ALU.add, ALU.add))
            step(dve.tensor_tensor(prod[:, :, :], over(v["drop_rank"], E), over_j(empty_excl),
                                   ALU.is_ge))
            step(dve.tensor_tensor(prod[:, :, :], prod[:, :, :], over_j(filled), ALU.mult))
            step(dve.tensor_reduce(v["slot_drop"], prod[:, :, :].rearrange("p e j -> p j e"), AX_X,
                                   ALU.add))
            step(dve.tensor_tensor(v["slot_drop"], v["slot_drop"], v["drop_rank"], ALU.add))
            step(dve.tensor_tensor(v["slot_diff"], v["slot_keep"], v["slot_drop"], ALU.subtract))
            step(dve.tensor_tensor(v["slot_diff"], v["slot_diff"], v["keep"], ALU.mult))
            step(dve.tensor_tensor(v["slot_i"], v["slot_diff"], v["slot_drop"], ALU.add))
            step(dve.tensor_scalar(v["a_i"], v["slot_i"], P.bit_length() - 1, None,
                                   ALU.logical_shift_right), False)
            step(dve.tensor_scalar(v["b_i"], v["slot_i"], P - 1, None, ALU.bitwise_and))
            step(dve.tensor_copy(a_b[:, :], v["a_i"]), False)
            step(dve.tensor_copy(b_b[:, :], v["b_i"]))
            dve.wait_ge(s_index, 2)

            def weigh_a(a0, a1):
                step(dve.tensor_tensor(oh_a[:, a0:a1, :], over(a_b[:, :], a1 - a0), index_b[:, a0:a1, :],
                                       ALU.is_equal))
                step(dve.tensor_scalar(oh_aw[:, 0, a0:a1, :], oh_a[:, a0:a1, :], lane[:, 0:1], None,
                                       ALU.mult), False)
                dve.tensor_tensor(oh_aw[:, 1, a0:a1, :], oh_a[:, a0:a1, :],
                                  over(index_j[:, :], a1 - a0), ALU.mult).then_inc(s_oh, 1)

            def row_numbers(a0, a1, inv):
                n = a1 - a0
                f, i, bi, bf = (w[:, a0:a1] for w in (tok_f, tok_i, batch_i, batch_f))
                step(dve.tensor_copy(tok_j[:, a0:a1], inv[:, n:2 * n]))
                step(dve.scalar_tensor_tensor(f, inv[:, 0:n], float(J), tok_j[:, a0:a1],
                                              ALU.mult, ALU.add))
                step(dve.tensor_copy(i, f))
                step(dve.tensor_scalar(bi, i, T.bit_length() - 1, None, ALU.logical_shift_right))
                step(dve.tensor_copy(bf, bi))
                step(dve.scalar_tensor_tensor(row_cur[:, a0:a1], f, 1.0, bf, ALU.add, ALU.add), False)
                step(dve.tensor_tensor(row_prev[:, a0:a1], f, bf, ALU.add), False)
                dve.tensor_copy(row_out[:, a0:a1], i).then_inc(s_rows, 1)

            step(dve.tensor_tensor(oh_b[:, :, :], over(b_b[:, :], P), index_b[:, :, :], ALU.is_equal),
                 False)
            weigh_a(0, ST)
            step(dve.tensor_tensor(mask[:, :].rearrange("p (e t) -> p e t", t=ST),
                                   slot_pos[:, :].unsqueeze(1).to_broadcast([P, E, ST]),
                                   filled[:, :].unsqueeze(2).to_broadcast([P, E, ST]), ALU.is_lt), False)
            dve.wait_ge(s_inv, 1)
            row_numbers(0, ST, inv_ps[0])
            for k in range(KD):
                dve.wait_ge(s_wrhi, k + 1)
                dve.tensor_tensor(wr_lo[:, k, :], (tx[0], td[0], tx[1], td[1])[k][:, :],
                                  wr_hi[:, k, :].bitcast(F32), ALU.subtract).then_inc(s_wrlo, 1)
            weigh_a(ST, A)

            def split_weight(n):
                dve.wait_ge(s_whi, n + 1)
                dve.tensor_tensor(weight_dst(n, wk_lo, wv_lo), raw[:, n % RAW_SLOTS, :],
                                  weight_dst(n, wk_hi, wv_hi).bitcast(F32), ALU.subtract).then_inc(s_wlo, 1)

            def diff(e, t):
                dve.wait_ge(s_prev[t], 16 * (e + 1))
                dve.wait_ge(s_cur[e % 2][t], 16 * (e // 2 + 1))
                dve.tensor_tensor(dxrow[:, t, :], dxrow[:, t, :], xrow[:, e % 2, t, :],
                                  ALU.subtract).then_inc(s_dx, 1)

            def mix_sum(e, k, i):
                n = e * KD + k
                v = 2 * n + i
                if i == 0:
                    dve.wait_ge(s_xT, n + 1)
                if v >= MIX_SLOTS:
                    dve.wait_ge(s_xlo, v - MIX_SLOTS + 1)
                dve.scalar_tensor_tensor(mix[:, v % MIX_SLOTS, :], td[n % 2][:, :],
                                         (maar, maak)[i][:, k:k + 1], xT[:, n % 2, :],
                                         ALU.mult, ALU.add).then_inc(s_mix, 1)

            def split_mix(e, k, i):
                v = (e * KD + k) * 2 + i
                dve.wait_ge(s_xhi, v + 1)
                dve.tensor_tensor((xr_lo, xk_lo)[i][:, k, :], mix[:, v % MIX_SLOTS, :],
                                  (xr_hi, xk_hi)[i][:, k, :].bitcast(F32), ALU.subtract).then_inc(s_xlo, 1)

            def square(n):
                dve.wait_ge(s_relu, n + 1)
                h = hid[:, n % H_SLOTS, :]
                dve.tensor_tensor(h, h, h, ALU.mult).then_inc(s_sq, 1)

            def split_hidden(n):
                dve.wait_ge(s_hhi, n + 1)
                dve.tensor_tensor(h_lo[:, n % KF, :], hid[:, n % H_SLOTS, :],
                                  h_hi[:, n % KF, :].bitcast(F32), ALU.subtract).then_inc(s_hlo, 1)

            def result(e, t):
                n = e * ST + t
                dve.wait_ge(s_D, n + 1)
                dve.scalar_tensor_tensor(gate[:, t, :], acc[t][:, :], mask[:, n:n + 1], gate[:, t, :],
                                         ALU.mult, ALU.mult).then_inc(s_y, 1)
                dve.wait_ge(s_y, n + 1)
                dve.tensor_tensor(xrow[:, e % 2, t, :], gate[:, t, :], xrow[:, e % 2, t, :],
                                  ALU.add).then_inc(s_res, 1)

            def mixes(e, after):
                mix_sum(e, 0, 0)
                mix_sum(e, 0, 1)
                mix_sum(e, 1, 0)
                split_mix(e, 0, 0)
                mix_sum(e, 1, 1)
                split_mix(e, 0, 1)
                split_mix(e, 1, 0)
                split_mix(e, 1, 1)
                after[0]()
                for k in (2, 3):
                    mix_sum(e, k, 0)
                    mix_sum(e, k, 1)
                    split_mix(e, k, 0)
                    split_mix(e, k, 1)
                    after[k - 1]()

            split_weight(0)
            split_weight(1)
            for t in range(ST):
                diff(0, t)
            split_weight(2)
            dve.wait_ge(s_inv, 2)
            row_numbers(ST, A, inv_ps[1])
            dve.wait_ge(s_maa, 32)
            mixes(0, [lambda: split_weight(3), lambda: None, lambda: None])
            for e in range(E):
                for m in range(KF):
                    n = e * KF + m
                    square(n)
                    if m > 0:
                        split_hidden(n - 1)
                    if m < NCH - KD:
                        split_weight(e * NCH + KD + m)
                    elif e + 1 < E and m < NCH - KD + 2:
                        for t in (0, 1):
                            diff(e + 1, 2 * (m - (NCH - KD)) + t)
                split_hidden(n)
                if e + 1 == E:
                    for t in range(ST):
                        result(e, t)
                    continue
                w = (e + 1) * NCH
                mixes(e + 1, [lambda: (split_weight(w), result(e, 0)),
                              lambda: (split_weight(w + 1), result(e, 1)),
                              lambda: (split_weight(w + 2), result(e, 2))])
                split_weight(w + 3)
                result(e, 3)

        @block.tensor
        def _(pe):
            def transpose_w_recept():
                for k in range(KD):
                    bank = (tx[0], td[0], tx[1], td[1])[k]
                    for r in range(KD):
                        if k == 0:
                            pe.wait_ge(s_wrec[r], 16)
                        last = pe.transpose(bank[:, r * P:(r + 1) * P], wr_raw[:, r, k * P:(k + 1) * P],
                                            ident[:, :])
                    last.then_inc(s_wrT, 1)

            def transposes(e, k):
                n = e * KD + k
                if n >= 2:
                    pe.wait_ge(s_mix, 2 * (n - 1))
                cols = slice(k * P, (k + 1) * P)
                for t in range(ST):
                    if k == 0:
                        pe.wait_ge(s_dx, e * ST + t + 1)
                    pe.transpose(tx[n % 2][:, t * P:(t + 1) * P], xrow[:, e % 2, t, cols], ident[:, :])
                    last = pe.transpose(td[n % 2][:, t * P:(t + 1) * P], dxrow[:, t, cols], ident[:, :])
                last.then_inc(s_T, 1)

            def triple(bank, hi, lo, m_hi, m_lo, first, last):
                pe.matmul(bank[:, :], hi, m_hi, start=first, stop=False)
                pe.matmul(bank[:, :], hi, m_lo, start=False, stop=False)
                return pe.matmul(bank[:, :], lo, m_hi, start=False, stop=last)

            def receptance(e, t):
                if e > 0:
                    pe.wait_ge(s_y, (e - 1) * ST + t + 1)
                for k in range(KD):
                    if t == 0:
                        pe.wait_ge(s_xlo, (e * KD + k) * 2 + 1)
                    rows = slice(t * P, (t + 1) * P)
                    mm = triple(acc[t], xr_hi[:, k, rows], xr_lo[:, k, rows], wr_hi[:, k, :], wr_lo[:, k, :],
                                k == 0, k == KD - 1)
                mm.then_inc(s_R, 1)

            def up(e, m):
                n = e * KF + m
                if m < ST:
                    pe.wait_ge(s_gate, e * ST + m + 1)
                else:
                    pe.wait_ge(s_relu, n - 3)
                cols = slice(m * P, (m + 1) * P)
                for k in range(KD):
                    if m == 0:
                        pe.wait_ge(s_wlo, e * NCH + k + 1)
                        pe.wait_ge(s_xlo, (e * KD + k) * 2 + 2)
                    mm = triple(acc[m % 4], wk_hi[:, k, cols], wk_lo[:, k, cols], xk_hi[:, k, :],
                                xk_lo[:, k, :], k == 0, k == KD - 1)
                mm.then_inc(s_U, 1)

            def down(e, t):
                pe.wait_ge(s_relu, e * KF + 5 + t)
                rows = slice(t * P, (t + 1) * P)
                for k in range(KF):
                    if t == 0:
                        if k % FPC == 0:
                            pe.wait_ge(s_wlo, e * NCH + KD + k // FPC + 1)
                        pe.wait_ge(s_hlo, e * KF + k + 1)
                    mm = triple(acc[t], h_hi[:, k, rows], h_lo[:, k, rows], wv_hi[:, k, :], wv_lo[:, k, :],
                                k == 0, k == KF - 1)
                mm.then_inc(s_D, 1)

            pe.wait_ge(s_const, N_CONST)
            pe.wait_ge(s_route, ROUTE_TOTALS)
            pe.matmul(count_ps[:, 0:E], tri[:, :], totals[:, :], start=True, stop=True)
            pe.matmul(count_ps[:, E:2 * E], ones[:, :], totals[:, :], start=True,
                      stop=True).then_inc(s_count, 1)
            transpose_w_recept()
            pe.wait_ge(s_route, ROUTE_DROPS)
            pe.matmul(drop_ps[:, 0:1], tri[:, :], drop_total[:, :], start=True, stop=True).then_inc(s_count, 1)
            for n, (a0, a1) in enumerate(((0, ST), (ST, A))):
                pe.wait_ge(s_oh, n + 1)
                for j in range(J):
                    mm = pe.matmul(inv_ps[n][:, 0:2 * (a1 - a0)], oh_b[:, :, j], oh_aw[:, :, a0:a1, j],
                                   start=(j == 0), stop=(j == J - 1))
                mm.then_inc(s_inv, 1)

            pe.wait_ge(s_wrlo, KD)
            for k in range(KD):
                transposes(0, k)
            for t in range(ST):
                receptance(0, t)
            for e in range(E):
                for m in range(KF):
                    up(e, m)
                if e + 1 == E:
                    for t in range(ST):
                        down(e, t)
                    continue
                transposes(e + 1, 0)
                transposes(e + 1, 1)
                for t in range(ST):
                    down(e, t)
                    if t < 2:
                        transposes(e + 1, 2 + t)
                for t in range(ST):
                    receptance(e + 1, t)


def kernel(**inputs):
    import numpy as _np
    import concourse.bacc as _bacc
    from concourse import mybir as _mybir
    from concourse.bass_utils import run_bass_kernel_spmd as _run

    x = _np.asarray(inputs["x"])
    cond = _np.asarray(inputs["cond_1024"])
    B, T, D = x.shape
    arrays = {
        "xs": _np.concatenate([cond[:, None, :], x], axis=1).reshape(B * (T + 1), D),
        "token_ids": _np.ascontiguousarray(inputs["itok_BxS_2_50255"]),
        "time_maa_k": _np.ascontiguousarray(inputs["L0_cond_time_maa_k"]),
        "time_maa_r": _np.ascontiguousarray(inputs["L0_cond_time_maa_r"]),
        "w_recept": _np.ascontiguousarray(inputs["L0_cond_w_recept"]),
        "w_key": _np.ascontiguousarray(inputs["L0_cond_w_key"]),
        "w_value": _np.ascontiguousarray(inputs["L0_cond_w_value"]),
    }
    nc = _bacc.Bacc("TRN2", target_bir_lowering=False, num_devices=1)
    args = [nc.dram_tensor(name, a.shape, _mybir.dt.from_np(a.dtype), kind="ExternalInput").ap()
            for name, a in arrays.items()]
    out = nc.dram_tensor("out", (B * T, D), _mybir.dt.float32, kind="ExternalOutput").ap()
    moe_token_shift(nc, *args, out)
    r = _run(nc, [arrays], core_ids=[0])
    return r.results[0]["out"].reshape(B, T, D)
```

```python
import math
from contextlib import ExitStack

import concourse.bass as bass
from concourse import mybir

F32 = mybir.dt.float32
F32R = mybir.dt.float32r
BF16 = mybir.dt.bfloat16
I32 = mybir.dt.int32
ALU = mybir.AluOpType
ACT = mybir.ActivationFunctionType
AX_X = mybir.AxisListType.X

HASH_PRIME = 5099
P = 128
RAW_SLOTS = 3
H_SLOTS = 3
X_SLOTS = 3
BLOCK = 32
MIX_SLOTS = 5


def moe_token_shift(nc, x, pairs, xs_t, ids, maa_k, maa_r, w_recept_t, w_key, w_value, out, gates):
    B, T = ids.shape
    E, D, F = w_key.shape
    N = B * T
    C = N // E
    J = N // P
    ST = C // P
    A = N // P
    G = N // C
    Q = P // BLOCK
    DQ = D // Q
    SB = C // BLOCK
    GB = T // C
    KD, KF = D // P, F // P
    assert E & (E - 1) == 0 and E * C == N and T & (T - 1) == 0 and T % J == 0 and T % C == 0
    assert D == 512 and F == 2 * D and ST == KD == Q == 4 and KF == 8 and G == 16
    assert DQ == KD * BLOCK
    unhash = pow(HASH_PRIME, -1, E)
    CHUNK = F
    FPC = CHUNK // D
    NCH = KD + KF // FPC
    N_CONST = 8
    PE_COUNT, PE_DROP, PE_INVERT, PE_SPREAD = 11, 21, 40, 42
    DVE_ROUTE = (6, 8, 13, 15, 17, 18, 23, 24, 25, 27, 28, 29, 31, 32, 33, 35, 36, 41, 43)
    POOL_DIFF = [g * KD + k for g in range(2, 11) for k in (1, 3)]
    FIRST_XK = (60, 61, 62, 63)
    FIRST_KEY = (46, 49, 52, 55)

    with ExitStack() as ctx:
        def sb(name, shape, dt):
            return ctx.enter_context(nc.sbuf_tensor(name, shape, dt))

        def psum(name):
            return ctx.enter_context(nc.psum_tensor(name, [P, 512], F32))

        def sem(name):
            return ctx.enter_context(nc.semaphore(name))

        ident = sb("ident", [P, P], F32)
        maar = sb("maar", [P, KD], F32)
        maak = sb("maak", [P, KD], F32)
        sigmoid_table = sb("sigmoid_table", [P, 1], F32)
        mask = sb("mask", [P, A], F32)
        row_tok = sb("row_tok", [P, A], I32)
        row_pair = sb("row_pair", [P, E * SB], I32)
        raw = sb("raw", [P, RAW_SLOTS, CHUNK], F32)
        gate = sb("gate", [P, ST, D], F32)

        phase1_words = []
        with ExitStack() as phase1:
            def p1(name, shape, dt=F32):
                phase1_words.append(math.prod(shape[1:]))
                return phase1.enter_context(nc.sbuf_tensor(name, shape, dt))

            xT = p1("xT", [P, X_SLOTS, KD, 1 + C])
            wr_raw = p1("wr_raw", [P, KD, D])
            wr_hi = p1("wr_hi", [P, KD, D], F32R)
            wr_lo = p1("wr_lo", [P, KD, D], F32R)
            mix = p1("mix", [P, MIX_SLOTS, C])
            xr_hi = p1("xr_hi", [P, 2, KD, C], F32R)
            xr_lo = p1("xr_lo", [P, 2, KD, C], F32R)
        pair_odd = sb("pair_odd", [P, SB, 2 * DQ], F32)
        wv_hi = sb("wv_hi", [P, KF, D], F32R)
        wv_lo = sb("wv_lo", [P, KF, D], F32R)
        hid = sb("hid", [P, H_SLOTS, C], F32)
        h_hi = sb("h_hi", [P, KF, C], F32R)
        h_lo = sb("h_lo", [P, KF, C], F32R)
        sb("phase1_rest", [P, sum(phase1_words) - 4 * KF * C - H_SLOTS * C - SB * 2 * DQ], F32)

        with ExitStack() as routing:
            def rt(name, shape, dt=F32):
                return routing.enter_context(nc.sbuf_tensor(name, shape, dt))

            residue = rt("residue", [P, E], I32)
            residue_b = rt("residue_b", [P, E], BF16)
            segment = rt("segment", [P, E, J], BF16)
            onehot = rt("onehot", [P, E, J], BF16)
            cum = rt("cum", [P, E, J])
            prod = rt("prod", [P, E, J])
            tri = rt("tri", [P, P], BF16)
            ones = rt("ones", [P, P], BF16)
            totals = rt("totals", [P, E], BF16)
            drop_total = rt("drop_total", [P, 1], BF16)
            index_b = rt("index_b", [P, P, J], BF16)
            index_j = rt("index_j", [P, J], BF16)
            oh_b = rt("oh_b", [P, P, J], BF16)
            oh_a = rt("oh_a", [P, A, J], BF16)
            oh_aw = rt("oh_aw", [P, 2, A, J], BF16)
            b_b = rt("b_b", [P, J], BF16)
            a_b = rt("a_b", [P, J], BF16)
            wide = {name: rt(name, [P, J], dt) for name, dt in (
                ("id_i", I32), ("id_low", I32), ("id_low_b", BF16), ("e_i", I32), ("e_f", F32),
                ("slot_keep", F32), ("within", F32), ("keep", F32), ("drop", F32), ("drop_cum", F32),
                ("drop_rank", F32), ("slot_drop", F32), ("slot_diff", F32), ("slot_i", I32),
                ("b_i", I32), ("a_i", I32), ("ones_j", F32))}
            slot_base = rt("slot_base", [P, E])
            off = rt("off", [P, E])
            filled = rt("filled", [P, E])
            empty = rt("empty", [P, E])
            empty_incl = rt("empty_incl", [P, E])
            empty_excl = rt("empty_excl", [P, E])
            lane = rt("lane", [P, 1])
            slot_pos = rt("slot_pos", [P, ST])
            select = rt("select", [P, Q, Q, BLOCK])
            lane_i = rt("lane_i", [P, 1], I32)
            quarter_i = rt("quarter_i", [P, 1], I32)
            quarter = rt("quarter", [P, 1])
            tok_j = rt("tok_j", [P, A])
            tok_f = rt("tok_f", [P, A])
        id_i = wide["id_i"][:, :]
        wk_hi = sb("wk_hi", [P, KD, F], F32R)
        wk_lo = sb("wk_lo", [P, KD, F], F32R)
        xrow = sb("xrow", [P, ST, D], F32)
        pair_even = sb("pair_even", [P, SB, 2 * DQ], F32)
        prev_t = sb("prev_t", [P, 2, C], F32)
        cur_t = sb("cur_t", [P, 2, C], F32)
        xk_hi = sb("xk_hi", [P, KD, C], F32R)
        xk_lo = sb("xk_lo", [P, KD, C], F32R)

        pair = [pair_even, pair_odd]

        acc = [psum(f"acc{i}") for i in range(4)]
        rt_bank = psum("rt_bank")
        count_ps = rt_bank[:, 0:2 * E]
        drop_ps = rt_bank[:, 2 * E:2 * E + 1]
        inv_ps = rt_bank[:, P:P + 2 * A]
        tok_ps = rt_bank[:, 2 * P:2 * P + Q * A]
        s_ids = sem("s_ids")
        s_maar = sem("s_maar")
        s_maak = sem("s_maak")
        s_wrec = [sem(f"s_wrec{k}") for k in range(KD)]
        s_raw = [sem(f"s_raw{i}") for i in range(RAW_SLOTS)]
        s_x = [[sem(f"s_x{b}{k}") for k in range(KD)] for b in range(X_SLOTS)]
        s_store = [sem(f"s_store{t}") for t in range(ST)]
        s_cur = [sem(f"s_cur{t}") for t in range(ST)]
        s_pair = [sem(f"s_pair{b}") for b in range(2)]
        s_gat = [sem(f"s_gat{t}") for t in range(ST)]
        s_scat = [sem(f"s_scat{t}") for t in range(ST)]
        s_zero = sem("s_zero")
        s_ident = sem("s_ident")
        s_table = sem("s_table")
        s_const = sem("s_const")
        s_index = sem("s_index")
        s_route = sem("s_route")
        s_totals = sem("s_totals")
        s_drops = sem("s_drops")
        s_count = sem("s_count")
        s_oh = sem("s_oh")
        s_inv = sem("s_inv")
        s_tok = sem("s_tok")
        s_spread = sem("s_spread")
        s_rows = sem("s_rows")
        s_wrhi = sem("s_wrhi")
        s_wrlo = sem("s_wrlo")
        s_diff = sem("s_diff")
        s_pool_diff = sem("s_pool_diff")
        s_mix = sem("s_mix")
        s_rhi = sem("s_rhi")
        s_rlo = sem("s_rlo")
        s_R = sem("s_R")
        s_sig = sem("s_sig")
        s_whi = sem("s_whi")
        s_wlo = sem("s_wlo")
        s_block = sem("s_block")
        s_xdiff = sem("s_xdiff")
        s_xk = sem("s_xk")
        s_xhi = sem("s_xhi")
        s_xlo = sem("s_xlo")
        s_U = sem("s_U")
        s_relu = sem("s_relu")
        s_sq = sem("s_sq")
        s_hhi = sem("s_hhi")
        s_hlo = sem("s_hlo")
        s_D = sem("s_D")
        s_y = sem("s_y")
        s_res = sem("s_res")

        block = ctx.enter_context(nc.Block())

        @block.sync
        def _(sp):
            def load_group(g, k):
                if g >= X_SLOTS:
                    sp.wait_ge(s_mix, KD * (g - X_SLOTS) + k + 1)
                first = g * C + g // GB
                sp.dma_start(xT[:, g % X_SLOTS, k, :],
                             xs_t[k * P:(k + 1) * P, first:first + 1 + C]).then_inc(
                                 s_x[g % X_SLOTS][k], 16)

            def store_gates(g):
                for t in range(ST):
                    sp.wait_ge(s_sig, g * ST + t + 1)
                    sp.dma_start(gates[g * C + t * P:g * C + (t + 1) * P, :],
                                 gate[:, t, :]).then_inc(s_store[t], 16)

            key = w_key.rearrange("e (k p) f -> e k p f", p=P)
            value = w_value.rearrange("e (c i p) d -> e c p i d", p=P, i=FPC)

            def load_weight(n):
                e, c = divmod(n, NCH)
                if n >= RAW_SLOTS:
                    sp.wait_ge(s_wlo, n - RAW_SLOTS + 1)
                slot = raw[:, n % RAW_SLOTS, :]
                if c < KD:
                    sp.dma_start(slot, key[e, c]).then_inc(s_raw[n % RAW_SLOTS], 16)
                else:
                    sp.dma_start(slot.rearrange("p (i d) -> p i d", i=FPC),
                                 value[e, c - KD]).then_inc(s_raw[n % RAW_SLOTS], 16)

            for k in range(KD):
                load_group(0, k)
                if k == 0:
                    sp.dma_start(maar[:, :], maa_r[:, :]).then_inc(s_maar, 16)
                sp.dma_start(wr_raw[:, k, :], w_recept_t[k * P:(k + 1) * P, :]).then_inc(s_wrec[k], 16)
            for k in range(KD):
                load_group(1, k)
            sp.dma_start(id_i, ids.rearrange("b (q j) -> (b q) j", j=J)).then_inc(s_ids, 16)
            sp.dma_start(maak[:, :], maa_k[:, :]).then_inc(s_maak, 16)
            for n in range(RAW_SLOTS):
                load_weight(n)
            for k in range(KD):
                load_group(2, k)
            for g in range(G):
                if g + X_SLOTS < G:
                    for k in range(KD):
                        load_group(g + X_SLOTS, k)
                for c in range(KD):
                    if FIRST_KEY[c] // KD == g:
                        load_weight(RAW_SLOTS + c)
                store_gates(g)
            for n in range(RAW_SLOTS + KD, E * NCH):
                load_weight(n)

        @block.gpsimd
        def _(pool):
            small_ints = {"allow_small_or_imprecise_dtypes": True}
            pool.memset(ident[:, :], 0.0).then_inc(s_zero, 1)
            pool.wait_ge(s_zero, 1)
            pool.affine_select(out=ident[:, :], in_=ident[:, :], compare_op=ALU.not_equal, fill=1.0,
                               base=0, pattern=[[-1, P]], channel_multiplier=1).then_inc(s_ident, 1)
            pool.iota(residue[:, :], [[unhash, E]], base=0, channel_multiplier=0).then_inc(s_table, 1)
            pool.memset(segment[:, :, :], 1.0).then_inc(s_zero, 1)
            pool.wait_ge(s_zero, 2)
            pool.memset(segment[:, :, 0:1], 0.0).then_inc(s_table, 1)
            pool.memset(tri[:, :], 1.0).then_inc(s_zero, 1)
            pool.memset(ones[:, :], 1.0).then_inc(s_const, 1)
            pool.wait_ge(s_zero, 3)
            pool.affine_select(out=tri[:, :], in_=tri[:, :], compare_op=ALU.is_gt, fill=0.0,
                               base=0, pattern=[[1, P]], channel_multiplier=-1).then_inc(s_const, 1)
            pool.iota(slot_base[:, :], [[C, E]], base=-1, channel_multiplier=0,
                      **small_ints).then_inc(s_const, 1)
            pool.memset(wide["ones_j"][:, :], 1.0).then_inc(s_const, 1)
            pool.iota(lane[:, :], [[0, 1]], base=0, channel_multiplier=1,
                      **small_ints).then_inc(s_const, 1)
            pool.iota(lane_i[:, :], [[0, 1]], base=0, channel_multiplier=1).then_inc(s_const, 1)
            pool.iota(slot_pos[:, :], [[P, ST]], base=0, channel_multiplier=1,
                      **small_ints).then_inc(s_const, 1)
            pool.iota(index_j[:, :], [[1, J]], base=0, channel_multiplier=0,
                      **small_ints).then_inc(s_const, 1)
            pool.iota(index_b[:, :, :], [[1, P], [0, J]], base=0, channel_multiplier=0,
                      **small_ints).then_inc(s_index, 1)

            def gather(table, e, t, rows, dst, s):
                a = e * ST + t
                pool.indirect_dma_start(dst, None, table,
                                        bass.IndirectOffsetOnAxis(rows[:, a:a + 1], 0)).then_inc(s, 16)

            def gather_cur(e, t):
                if e > 0:
                    pool.wait_ge(s_scat[t], 16 * e)
                gather(x, e, t, row_tok, xrow[:, t, :], s_cur[t])

            def gather_gate(e, t):
                if e > 0:
                    pool.wait_ge(s_res, (e - 1) * ST + t + 1)
                gather(gates, e, t, row_tok, gate[:, t, :], s_gat[t])

            def gather_pairs(e):
                if e >= 2:
                    pool.wait_ge(s_block, 2 * KD * (e - 1))
                for i in range(SB):
                    a = e * SB + i
                    pool.indirect_dma_start(pair[e % 2][:, i, :], None, pairs,
                                            bass.IndirectOffsetOnAxis(row_pair[:, a:a + 1], 0)).then_inc(
                                                s_pair[e % 2], 16)

            def scatter(e, t):
                a = e * ST + t
                pool.wait_ge(s_res, e * ST + t + 1)
                pool.indirect_dma_start(out, bass.IndirectOffsetOnAxis(row_tok[:, a:a + 1], 0),
                                        xrow[:, t, :], None).then_inc(s_scat[t], 16)

            for n in POOL_DIFF:
                g, k = divmod(n, KD)
                pool.wait_ge(s_x[g % X_SLOTS][k], 16 * (g // X_SLOTS + 1))
                if n >= MIX_SLOTS:
                    pool.wait_ge(s_rlo, n - MIX_SLOTS + 1)
                x_chunk = xT[:, g % X_SLOTS, k, :]
                pool.tensor_tensor(mix[:, n % MIX_SLOTS, :], x_chunk[:, 0:C], x_chunk[:, 1:1 + C],
                                   ALU.subtract).then_inc(s_pool_diff, 1)
            pool.wait_ge(s_rows, 1)
            gather_pairs(0)
            for t in range(ST):
                gather_cur(0, t)
            pool.wait_ge(s_mix, G * KD)
            gather_pairs(1)
            for t in range(ST):
                pool.wait_ge(s_store[t], 16 * G)
            for t in range(ST):
                gather_gate(0, t)
            for e in range(E):
                if e + 2 < E:
                    gather_pairs(e + 2)
                for t in range(ST):
                    scatter(e, t)
                    if e + 1 < E:
                        gather_gate(e + 1, t)
                        if t > 0:
                            gather_cur(e + 1, t - 1)
                if e + 1 < E:
                    gather_cur(e + 1, ST - 1)
            for t in range(ST):
                pool.wait_ge(s_scat[t], 16 * E)

        def weight_dst(n, key, value):
            c = n % NCH
            return key[:, c, :] if c < KD else value[:, (c - KD) * FPC:(c - KD + 1) * FPC, :].rearrange(
                "p i d -> p (i d)")

        @block.scalar
        def _(act):
            def split_xr(g, k):
                n = g * KD + k
                act.wait_ge(s_mix, n + 1)
                if g >= 2:
                    act.wait_ge(s_R, ST * (g - 1))
                act.copy(xr_hi[:, g % 2, k, :], mix[:, n % MIX_SLOTS, :]).then_inc(s_rhi, 1)

            def sigmoids(g):
                for t in range(ST):
                    act.wait_ge(s_R, g * ST + t + 1)
                    if g > 0:
                        act.wait_ge(s_store[t], 16 * g)
                    act.activation(gate[:, t, :], acc[t][:, :], ACT.Sigmoid).then_inc(s_sig, 1)

            def split_weight(n):
                e, c = divmod(n, NCH)
                act.wait_ge(s_raw[n % RAW_SLOTS], 16 * (n // RAW_SLOTS + 1))
                if n == 0:
                    act.wait_ge(s_rows, 1)
                if e > 0 and c == 0:
                    act.wait_ge(s_U, KF * e)
                if e > 0 and c == KD:
                    act.wait_ge(s_D, ST * e)
                act.copy(weight_dst(n, wk_hi, wv_hi), raw[:, n % RAW_SLOTS, :]).then_inc(s_whi, 1)

            def split_xk(e, k):
                act.wait_ge(s_xk, e * KD + k + 1)
                if e > 0:
                    act.wait_ge(s_U, KF * e)
                act.copy(xk_hi[:, k, :], prev_t[:, k % 2, :]).then_inc(s_xhi, 1)

            def relu(n):
                act.wait_ge(s_U, n + 1)
                if n >= H_SLOTS:
                    act.wait_ge(s_hlo, n - H_SLOTS + 1)
                act.activation(hid[:, n % H_SLOTS, :], acc[n % 4][:, :], ACT.Relu).then_inc(s_relu, 1)

            def split_hidden(n):
                act.wait_ge(s_sq, n + 1)
                act.copy(h_hi[:, n % KF, :], hid[:, n % H_SLOTS, :]).then_inc(s_hhi, 1)

            def split_w_recept(k):
                act.wait_ge(s_wrec[k], 16)
                act.copy(wr_hi[:, k, :], wr_raw[:, k, :]).then_inc(s_wrhi, 1)

            act.wait_ge(s_ident, 1)
            act.activation(sigmoid_table[:, :], ident[:, 0:1], ACT.Sigmoid)
            for k in range(KD):
                split_w_recept(k)
                split_xr(0, k)
            for g in range(G):
                for k in range(KD):
                    if g + 1 < G:
                        split_xr(g + 1, k)
                    if g * KD + k in FIRST_KEY:
                        split_weight(FIRST_KEY.index(g * KD + k))
                    if g * KD + k == FIRST_XK[0]:
                        split_xk(0, 0)
                        split_xk(0, 1)
                    elif g * KD + k in FIRST_XK[1:3]:
                        split_xk(0, 1 + FIRST_XK.index(g * KD + k))
                    if k == min(g, KD - 1):
                        sigmoids(g)

            for e in range(E):
                for m in range(KF):
                    n = e * KF + m
                    relu(n)
                    if m > 0:
                        split_hidden(n - 1)
                    if m < NCH - KD:
                        split_weight(e * NCH + KD + m)
                split_hidden(n)
                if e + 1 < E:
                    w = (e + 1) * NCH
                    for k in range(KD):
                        split_weight(w + k)
                        split_xk(e + 1, k)

        @block.vector
        def _(dve):
            steps = [0]
            v = {name: t[:, :] for name, t in wide.items()}

            def step(ins, read_next=True):
                steps[0] += 1
                ins.then_inc(s_route, 1)
                if read_next:
                    dve.wait_ge(s_route, steps[0])

            def over_j(w):
                return w[:, :].unsqueeze(2).to_broadcast([P, w.shape[1], J])

            def over(w, n):
                return w.unsqueeze(1).to_broadcast([P, n, w.shape[1]])

            def by_slots(w):
                return w[:, :, :].rearrange("p e j -> p j e")

            def routing():
                dve.wait_ge(s_table, 1)
                step(dve.tensor_scalar(residue[:, :], residue[:, :], E - 1, None, ALU.bitwise_and))
                step(dve.tensor_copy(residue_b[:, :], residue[:, :]), False)
                dve.wait_ge(s_ids, 16)
                step(dve.tensor_scalar(v["id_low"], v["id_i"], E - 1, None, ALU.bitwise_and))
                step(dve.tensor_copy(v["id_low_b"], v["id_low"]))
                step(dve.tensor_tensor(onehot[:, :, :], over(v["id_low_b"], E), over_j(residue_b),
                                       ALU.is_equal))
                yield
                dve.wait_ge(s_table, 2)
                dve.wait_ge(s_const, N_CONST)
                step(dve.tensor_tensor_scan(cum[:, :, :].rearrange("p e j -> p (e j)"),
                                            segment[:, :, :].rearrange("p e j -> p (e j)"),
                                            onehot[:, :, :].rearrange("p e j -> p (e j)"), 0.0,
                                            ALU.mult, ALU.add))
                dve.tensor_copy(totals[:, :], cum[:, :, J - 1]).then_inc(s_totals, 1)
                step(dve.tensor_scalar(v["e_i"], v["id_low"], HASH_PRIME % E, None, ALU.mult))
                step(dve.tensor_scalar(v["e_i"], v["e_i"], E - 1, None, ALU.bitwise_and))
                step(dve.tensor_copy(v["e_f"], v["e_i"]), False)
                yield
                dve.wait_ge(s_count, 1)
                step(dve.tensor_tensor(off[:, :], count_ps[:, 0:E], slot_base[:, :], ALU.add), False)
                step(dve.tensor_scalar(filled[:, :], count_ps[:, E:2 * E], float(C), None, ALU.min))
                step(dve.tensor_tensor(cum[:, :, :], cum[:, :, :], over_j(off), ALU.add), False)
                step(dve.tensor_scalar(empty[:, :], filled[:, :], -1.0, float(C), ALU.mult, ALU.add))
                yield
                step(dve.tensor_tensor(prod[:, :, :], cum[:, :, :], onehot[:, :, :], ALU.mult), False)
                step(dve.tensor_tensor_scan(empty_incl[:, :], v["ones_j"][:, 0:E], empty[:, :], 0.0,
                                            ALU.mult, ALU.add))
                yield
                step(dve.tensor_reduce(v["slot_keep"], by_slots(prod), AX_X, ALU.add), False)
                step(dve.tensor_tensor(empty_excl[:, :], empty_incl[:, :], empty[:, :], ALU.subtract))
                yield
                step(dve.scalar_tensor_tensor(v["within"], v["e_f"], -float(C), v["slot_keep"],
                                              ALU.mult, ALU.add))
                step(dve.tensor_scalar(v["drop"], v["within"], float(C), None, ALU.is_ge))
                step(dve.tensor_tensor_scan(v["drop_cum"], v["ones_j"], v["drop"], 0.0, ALU.mult,
                                            ALU.add))
                dve.tensor_copy(drop_total[:, :], v["drop_cum"][:, J - 1:J]).then_inc(s_drops, 1)
                step(dve.tensor_scalar(v["keep"], v["within"], float(C), None, ALU.is_lt), False)
                yield
                dve.wait_ge(s_count, 2)
                step(dve.tensor_scalar(v["drop_rank"], v["drop_cum"], drop_ps[:, 0:1], -1.0,
                                       ALU.add, ALU.add))
                step(dve.tensor_tensor(prod[:, :, :], over(v["drop_rank"], E), over_j(empty_excl),
                                       ALU.is_ge))
                yield
                step(dve.tensor_tensor(prod[:, :, :], prod[:, :, :], over_j(filled), ALU.mult))
                yield
                step(dve.tensor_reduce(v["slot_drop"], by_slots(prod), AX_X, ALU.add))
                yield
                step(dve.tensor_tensor(v["slot_drop"], v["slot_drop"], v["drop_rank"], ALU.add))
                step(dve.tensor_tensor(v["slot_diff"], v["slot_keep"], v["slot_drop"], ALU.subtract))
                step(dve.tensor_tensor(v["slot_diff"], v["slot_diff"], v["keep"], ALU.mult))
                step(dve.tensor_tensor(v["slot_i"], v["slot_diff"], v["slot_drop"], ALU.add))
                step(dve.tensor_scalar(v["a_i"], v["slot_i"], P.bit_length() - 1, None,
                                       ALU.logical_shift_right), False)
                step(dve.tensor_scalar(v["b_i"], v["slot_i"], P - 1, None, ALU.bitwise_and))
                step(dve.tensor_copy(a_b[:, :], v["a_i"]), False)
                step(dve.tensor_copy(b_b[:, :], v["b_i"]))
                yield
                dve.wait_ge(s_index, 1)
                for q in range(4):
                    js = slice(q * J // 4, (q + 1) * J // 4)
                    step(dve.tensor_tensor(oh_b[:, :, js], over(b_b[:, js], P), index_b[:, :, js],
                                           ALU.is_equal), q == 3)
                    yield
                step(dve.tensor_tensor(oh_a[:, :, :], over(a_b[:, :], A), index_b[:, 0:A, :],
                                       ALU.is_equal))
                yield
                step(dve.tensor_scalar(oh_aw[:, 0, :, :], oh_a[:, :, :], lane[:, 0:1], None,
                                       ALU.mult), False)
                yield
                dve.tensor_tensor(oh_aw[:, 1, :, :], oh_a[:, :, :], over(index_j[:, :], A),
                                  ALU.mult).then_inc(s_oh, 1)
                step(dve.tensor_tensor(mask[:, :].rearrange("p (e t) -> p e t", t=ST),
                                       slot_pos[:, :].unsqueeze(1).to_broadcast([P, E, ST]),
                                       filled[:, :].unsqueeze(2).to_broadcast([P, E, ST]), ALU.is_lt),
                     False)
                yield
                dve.wait_ge(s_ident, 1)
                step(dve.tensor_copy(select[:, :, :, :],
                                     ident[:, :].rearrange("p (b r) -> p b r", b=Q).unsqueeze(2)
                                     .to_broadcast([P, Q, Q, BLOCK])), False)
                dve.wait_ge(s_inv, 1)
                step(dve.tensor_copy(tok_j[:, :], inv_ps[:, A:2 * A]))
                dve.scalar_tensor_tensor(tok_f[:, :], inv_ps[:, 0:A], float(J), tok_j[:, :],
                                         ALU.mult, ALU.add).then_inc(s_tok, 1)
                dve.wait_ge(s_tok, 1)
                step(dve.tensor_copy(row_tok[:, :], tok_f[:, :]))
                step(dve.tensor_scalar(quarter_i[:, :], lane_i[:, :], BLOCK.bit_length() - 1, None,
                                       ALU.logical_shift_right))
                step(dve.tensor_copy(quarter[:, :], quarter_i[:, :]))
                yield
                dve.wait_ge(s_spread, 1)
                dve.tensor_scalar(row_pair[:, :].rearrange("p (a b) -> p b a", b=Q),
                                  tok_ps[:, :].rearrange("p (b a) -> p b a", b=Q), float(Q),
                                  quarter[:, 0:1], ALU.mult, ALU.add).then_inc(s_rows, 1)
                yield

            def mix_xr(g, k):
                n = g * KD + k
                slot = mix[:, n % MIX_SLOTS, :]
                here = xT[:, g % X_SLOTS, k, 1:1 + C]
                pool_diffs = sum(m <= n for m in POOL_DIFF)
                dve.wait_ge(s_x[g % X_SLOTS][k], 16 * (g // X_SLOTS + 1))
                if n in POOL_DIFF:
                    dve.wait_ge(s_pool_diff, pool_diffs)
                else:
                    if n >= MIX_SLOTS:
                        dve.wait_ge(s_rlo, n - MIX_SLOTS + 1)
                    dve.tensor_tensor(slot, xT[:, g % X_SLOTS, k, 0:C], here,
                                      ALU.subtract).then_inc(s_diff, 1)
                    dve.wait_ge(s_diff, n + 1 - pool_diffs)
                dve.scalar_tensor_tensor(slot, slot, maar[:, k:k + 1], here,
                                         ALU.mult, ALU.add).then_inc(s_mix, 1)

            def split_xr(n):
                g, k = divmod(n, KD)
                dve.wait_ge(s_rhi, n + 1)
                dve.tensor_tensor(xr_lo[:, g % 2, k, :], mix[:, n % MIX_SLOTS, :],
                                  xr_hi[:, g % 2, k, :].bitcast(F32), ALU.subtract).then_inc(s_rlo, 1)

            def split_weight(n):
                dve.wait_ge(s_whi, n + 1)
                dve.tensor_tensor(weight_dst(n, wk_lo, wv_lo), raw[:, n % RAW_SLOTS, :],
                                  weight_dst(n, wk_hi, wv_hi).bitcast(F32), ALU.subtract).then_inc(s_wlo, 1)

            def mix_xk(e, c):
                n = e * KD + c
                prev, cur = prev_t[:, c % 2, :], cur_t[:, c % 2, :]
                if c == 0:
                    dve.wait_ge(s_pair[e % 2], 16 * SB * (e // 2 + 1))
                if n >= 2:
                    dve.wait_ge(s_xlo, n - 1)
                for half, dst in enumerate((prev, cur)):
                    first = half * DQ + c * BLOCK
                    dve.transpose(dst.rearrange("p (s r) -> p s r", r=BLOCK),
                                  pair[e % 2][:, :, first:first + BLOCK]).then_inc(s_block, 1)
                dve.wait_ge(s_block, 2 * n + 2)
                dve.tensor_tensor(prev, prev, cur, ALU.subtract).then_inc(s_xdiff, 1)
                dve.wait_ge(s_xdiff, n + 1)
                dve.scalar_tensor_tensor(prev, prev, maak[:, c:c + 1], cur,
                                         ALU.mult, ALU.add).then_inc(s_xk, 1)

            def split_xk(e, k):
                dve.wait_ge(s_xhi, e * KD + k + 1)
                dve.tensor_tensor(xk_lo[:, k, :], prev_t[:, k % 2, :], xk_hi[:, k, :].bitcast(F32),
                                  ALU.subtract).then_inc(s_xlo, 1)

            def square(n):
                dve.wait_ge(s_relu, n + 1)
                h = hid[:, n % H_SLOTS, :]
                dve.tensor_tensor(h, h, h, ALU.mult).then_inc(s_sq, 1)

            def split_hidden(n):
                dve.wait_ge(s_hhi, n + 1)
                dve.tensor_tensor(h_lo[:, n % KF, :], hid[:, n % H_SLOTS, :],
                                  h_hi[:, n % KF, :].bitcast(F32), ALU.subtract).then_inc(s_hlo, 1)

            def result(e, t):
                n = e * ST + t
                dve.wait_ge(s_D, n + 1)
                dve.wait_ge(s_gat[t], 16 * (e + 1))
                dve.wait_ge(s_cur[t], 16 * (e + 1))
                dve.scalar_tensor_tensor(gate[:, t, :], acc[t][:, :], mask[:, n:n + 1], gate[:, t, :],
                                         ALU.mult, ALU.mult).then_inc(s_y, 1)
                dve.wait_ge(s_y, n + 1)
                dve.tensor_tensor(xrow[:, t, :], gate[:, t, :], xrow[:, t, :], ALU.add).then_inc(s_res, 1)

            route = routing()
            dve.wait_ge(s_maar, 16)
            mixed = 0
            for r in range(-KD, G * KD):
                n = r + KD
                while mixed < min(G * KD, n + (1 if n == 0 else min(KD, 2 + max(0, r) // KD))):
                    mix_xr(*divmod(mixed, KD))
                    mixed += 1
                if r < 0:
                    dve.wait_ge(s_wrhi, n + 1)
                    dve.tensor_tensor(wr_lo[:, n, :], wr_raw[:, n, :], wr_hi[:, n, :].bitcast(F32),
                                      ALU.subtract).then_inc(s_wrlo, 1)
                if n < G * KD:
                    split_xr(n)
                if r in FIRST_KEY:
                    split_weight(FIRST_KEY.index(r))
                if r in DVE_ROUTE:
                    next(route)
                if r == FIRST_XK[0]:
                    dve.wait_ge(s_maak, 16)
                    mix_xk(0, 0)
                    mix_xk(0, 1)
                elif r == FIRST_XK[1]:
                    split_xk(0, 0)
                    mix_xk(0, 2)
                elif r == FIRST_XK[2]:
                    split_xk(0, 1)
                    mix_xk(0, 3)
                elif r == FIRST_XK[3]:
                    split_xk(0, 2)
                    split_xk(0, 3)

            for e in range(E):
                for m in range(KF):
                    n = e * KF + m
                    square(n)
                    if m > 0:
                        split_hidden(n - 1)
                    if m < NCH - KD:
                        split_weight(e * NCH + KD + m)
                    elif m in (4, 6) and e + 1 < E:
                        mix_xk(e + 1, (m - 4) // 2)
                split_hidden(n)
                if e + 1 == E:
                    for t in range(ST):
                        result(e, t)
                    continue
                w = (e + 1) * NCH
                split_weight(w)
                split_xk(e + 1, 0)
                mix_xk(e + 1, 2)
                result(e, 0)
                split_weight(w + 1)
                split_xk(e + 1, 1)
                mix_xk(e + 1, 3)
                result(e, 1)
                split_weight(w + 2)
                split_xk(e + 1, 2)
                result(e, 2)
                split_weight(w + 3)
                split_xk(e + 1, 3)
                result(e, 3)

        @block.tensor
        def _(pe):
            def triple(bank, hi, lo, m_hi, m_lo, first, last):
                pe.matmul(bank[:, :], hi, m_hi, start=first, stop=False)
                pe.matmul(bank[:, :], hi, m_lo, start=False, stop=False)
                return pe.matmul(bank[:, :], lo, m_hi, start=False, stop=last)

            def receptance(g, k):
                pe.wait_ge(s_rlo, g * KD + k + 1)
                if g == 0:
                    pe.wait_ge(s_wrlo, k + 1)
                for t in range(ST):
                    if g > 0 and k == 0:
                        pe.wait_ge(s_sig, (g - 1) * ST + t + 1)
                    rows = slice(t * P, (t + 1) * P)
                    mm = triple(acc[t], xr_hi[:, g % 2, k, rows], xr_lo[:, g % 2, k, rows],
                                wr_hi[:, k, :], wr_lo[:, k, :], k == 0, k == KD - 1)
                    if k == KD - 1:
                        mm.then_inc(s_R, 1)

            def count():
                pe.wait_ge(s_totals, 1)
                pe.matmul(count_ps[:, 0:E], tri[:, :], totals[:, :], start=True, stop=True)
                pe.matmul(count_ps[:, E:2 * E], ones[:, :], totals[:, :], start=True,
                          stop=True).then_inc(s_count, 1)

            def count_drops():
                pe.wait_ge(s_drops, 1)
                pe.matmul(drop_ps[:, 0:1], tri[:, :], drop_total[:, :], start=True,
                          stop=True).then_inc(s_count, 1)

            def invert():
                pe.wait_ge(s_oh, 1)
                for j in range(J):
                    mm = pe.matmul(inv_ps[:, 0:2 * A], oh_b[:, :, j],
                                   oh_aw[:, :, :, j].rearrange("p h a -> p (h a)"),
                                   start=(j == 0), stop=(j == J - 1))
                mm.then_inc(s_inv, 1)

            def spread():
                pe.wait_ge(s_tok, 1)
                for b in range(Q):
                    mm = pe.matmul(tok_ps[:, b * A:(b + 1) * A],
                                   select[:, b, :, :].rearrange("p q r -> p (q r)"), tok_f[:, :],
                                   start=True, stop=True)
                mm.then_inc(s_spread, 1)

            def up(e, m):
                n = e * KF + m
                if m >= 4:
                    pe.wait_ge(s_relu, n - 3)
                elif e == 0:
                    pe.wait_ge(s_sig, (G - 1) * ST + m + 1)
                else:
                    pe.wait_ge(s_y, (e - 1) * ST + m + 1)
                cols = slice(m * P, (m + 1) * P)
                for k in range(KD):
                    if m == 0:
                        pe.wait_ge(s_wlo, e * NCH + k + 1)
                        pe.wait_ge(s_xlo, e * KD + k + 1)
                    mm = triple(acc[m % 4], wk_hi[:, k, cols], wk_lo[:, k, cols], xk_hi[:, k, :],
                                xk_lo[:, k, :], k == 0, k == KD - 1)
                mm.then_inc(s_U, 1)

            def down(e, t):
                pe.wait_ge(s_relu, e * KF + 5 + t)
                rows = slice(t * P, (t + 1) * P)
                for k in range(KF):
                    if t == 0:
                        if k % FPC == 0:
                            pe.wait_ge(s_wlo, e * NCH + KD + k // FPC + 1)
                        pe.wait_ge(s_hlo, e * KF + k + 1)
                    mm = triple(acc[t], h_hi[:, k, rows], h_lo[:, k, rows], wv_hi[:, k, :], wv_lo[:, k, :],
                                k == 0, k == KF - 1)
                mm.then_inc(s_D, 1)

            for g in range(G):
                for k in range(KD):
                    receptance(g, k)
                    for part, at in ((count, PE_COUNT), (count_drops, PE_DROP),
                                     (invert, PE_INVERT), (spread, PE_SPREAD)):
                        if g * KD + k == at:
                            part()
            for e in range(E):
                for m in range(KF):
                    up(e, m)
                for t in range(ST):
                    down(e, t)


def kernel(**inputs):
    import numpy as _np
    import concourse.bacc as _bacc
    from concourse import mybir as _mybir
    from concourse.bass_utils import run_bass_kernel_spmd as _run

    x = _np.asarray(inputs["x"])
    cond = _np.asarray(inputs["cond_1024"])
    w_key = _np.asarray(inputs["L0_cond_w_key"])
    B, T, D = x.shape
    E, _, F = w_key.shape
    xs = _np.concatenate([cond[:, None, :], x], axis=1)
    q, c, r = P // BLOCK, D // P, BLOCK
    arrays = {
        "x": _np.ascontiguousarray(x).reshape(B * T, D),
        "pairs": _np.stack([xs[:, :-1].reshape(B, T, q, D // q), x.reshape(B, T, q, D // q)],
                           axis=3).reshape(B * T * q, 2 * D // q),
        "xs_t": _np.ascontiguousarray(xs.reshape(B * (T + 1), D).T),
        "token_ids": _np.ascontiguousarray(inputs["itok_BxS_2_50255"]),
        "time_maa_k": _np.ascontiguousarray(
            _np.asarray(inputs["L0_cond_time_maa_k"]).reshape(q, c, r).transpose(0, 2, 1)).reshape(P, c),
        "time_maa_r": _np.ascontiguousarray(
            _np.asarray(inputs["L0_cond_time_maa_r"]).reshape(c, P).T),
        "w_recept_t": _np.ascontiguousarray(_np.asarray(inputs["L0_cond_w_recept"]).T),
        "w_key": _np.ascontiguousarray(
            w_key.reshape(E, q, c, r, F).transpose(0, 2, 1, 3, 4)).reshape(E, D, F),
        "w_value": _np.ascontiguousarray(inputs["L0_cond_w_value"]),
    }
    nc = _bacc.Bacc("TRN2", target_bir_lowering=False, num_devices=1)
    args = [nc.dram_tensor(name, a.shape, _mybir.dt.from_np(a.dtype), kind="ExternalInput").ap()
            for name, a in arrays.items()]
    out = nc.dram_tensor("out", (B * T, D), _mybir.dt.float32, kind="ExternalOutput").ap()
    gates = nc.dram_tensor("gates", (B * T, D), _mybir.dt.float32, kind="Internal").ap()
    moe_token_shift(nc, *args, out, gates)
    r = _run(nc, [arrays], core_ids=[0])
    return r.results[0]["out"].reshape(B, T, D)
```
